# Optimizing a Trainium2 kernel written in Bass

```python
import numpy as np
import jax
import jax.numpy as jnp

def _softmax(x, axis=-1):
    return jax.nn.softmax(x, axis=axis)

def _gelu(x):
    return jax.nn.gelu(x, approximate=True)

def _silu(x):
    return jax.nn.silu(x)

def _sigmoid(x):
    return jax.nn.sigmoid(x)

def _layernorm(x, axis=-1, eps=1e-05):
    m = jnp.mean(x, axis=axis, keepdims=True)
    v = jnp.var(x, axis=axis, keepdims=True)
    return (x - m) / jnp.sqrt(v + eps)

def _scatter_add(tgt, idx, src, axis=0):
    return tgt.at[idx].add(src)

def _segment_sum(src, seg, n):
    return jax.ops.segment_sum(src, seg, n)
kernel_name = 'mk_vit_tower_d1_tok_img1024_r4_315dd4'

def setup_inputs(seed: int=0):
    np.random.seed(seed)
    _w = jnp.asarray

    def _rec_inputs():
        import jax
        import jax.numpy as jnp
        _rk = jax.random.key(seed)
        x = -0.000356955 + 1 * jax.random.normal(jax.random.fold_in(_rk, 1), (32, 64, 64, 3), jnp.float32)
        return x
    x = _rec_inputs()

    def _L0_tok_setup():
        import jax, jax.numpy as jnp
        import numpy as np
        HIDDEN = 256
        PATCH = 16
        CHANNELS = 3
        PATCH_NDIM = CHANNELS * PATCH * PATCH
        INIT_STD = 1.0 / HIDDEN ** 0.5
        SCALE = 1.0 / (INIT_STD * PATCH_NDIM ** 0.5)
        key = jax.random.key(seed)
        k1, k2 = jax.random.split(key)
        image = jax.random.normal(k1, (128, 224, 224, CHANNELS), dtype=jnp.float32)
        weight = jax.random.normal(k2, (HIDDEN, PATCH_NDIM), dtype=jnp.float32) * INIT_STD
        return {'image': image, 'weight': weight}
    _L0_tok_all = _L0_tok_setup()
    _L0_tok_in = {k: v for k, v in _L0_tok_all.items() if k in ('weight',)}
    del _L0_tok_all

    def _L0_attn_setup():
        import jax, jax.numpy as jnp
        import numpy as np
        DIM = 256
        HEADS = 16
        DIM_HEAD = 64
        INNER = HEADS * DIM_HEAD
        SEQ = 1024
        BATCH = 1
        key = jax.random.key(seed)
        ks = jax.random.split(key, 6)
        s = 0.02
        return {'x': jax.random.normal(ks[0], (BATCH, SEQ, DIM), dtype=jnp.float32), 'Wq': jax.random.normal(ks[1], (DIM, INNER), dtype=jnp.float32) * s, 'Wk': jax.random.normal(ks[2], (DIM, INNER), dtype=jnp.float32) * s, 'Wv': jax.random.normal(ks[3], (DIM, INNER), dtype=jnp.float32) * s, 'Wo': jax.random.normal(ks[4], (INNER, DIM), dtype=jnp.float32) * s, 'bo': jax.random.normal(ks[5], (DIM,), dtype=jnp.float32) * s}
    _L0_attn_all = _L0_attn_setup()
    _L0_attn_in = {k: v for k, v in _L0_attn_all.items() if k in ('Wq', 'Wk', 'Wv', 'Wo', 'bo')}
    del _L0_attn_all

    def _L0_ffn_setup():
        import jax, jax.numpy as jnp
        import numpy as np
        B, S, H = (2, 256, 256)
        DFF = 512
        E = 8
        TOPK = 2

        def _expert_ffn(x, w1, b1, w2, b2, wg, bg, w3, b3):
            x1 = jnp.einsum('bsh,hf->bsf', x, w1) + b1
            x2 = jnp.einsum('bsh,hf->bsf', x, w2) + b2
            z = x1 * x2
            s = jax.nn.silu(jnp.einsum('bsf,fg->bsg', z, wg) + bg)
            return jnp.einsum('bsg,gh->bsh', s, w3) + b3
        key = jax.random.key(seed)
        ks = jax.random.split(key, 12)
        sc = 0.02
        return {'x': jax.random.normal(ks[0], (B, S, H), jnp.float32), 'gate_w': jax.random.normal(ks[1], (H, E), jnp.float32) * sc, 'gate_b': jnp.zeros((E,), jnp.float32), 'w1': jax.random.normal(ks[2], (E, H, DFF), jnp.float32) * sc, 'b1': jnp.zeros((E, DFF), jnp.float32), 'w2': jax.random.normal(ks[3], (E, H, DFF), jnp.float32) * sc, 'b2': jnp.zeros((E, DFF), jnp.float32), 'wg': jax.random.normal(ks[4], (E, DFF, DFF), jnp.float32) * sc, 'bg': jnp.zeros((E, DFF), jnp.float32), 'w3': jax.random.normal(ks[5], (E, DFF, H), jnp.float32) * sc, 'b3': jnp.zeros((E, H), jnp.float32)}
    _L0_ffn_all = _L0_ffn_setup()
    _L0_ffn_in = {k: v for k, v in _L0_ffn_all.items() if k in ('gate_w', 'gate_b', 'w1', 'b1', 'w2', 'b2', 'wg', 'bg', 'w3', 'b3')}
    del _L0_ffn_all
    return {'x': x, 'L0_tok_weight': _L0_tok_in['weight'], 'L0_attn_Wq': _L0_attn_in['Wq'], 'L0_attn_Wk': _L0_attn_in['Wk'], 'L0_attn_Wv': _L0_attn_in['Wv'], 'L0_attn_Wo': _L0_attn_in['Wo'], 'L0_attn_bo': _L0_attn_in['bo'], 'L0_ffn_gate_w': _L0_ffn_in['gate_w'], 'L0_ffn_gate_b': _L0_ffn_in['gate_b'], 'L0_ffn_w1': _L0_ffn_in['w1'], 'L0_ffn_b1': _L0_ffn_in['b1'], 'L0_ffn_w2': _L0_ffn_in['w2'], 'L0_ffn_b2': _L0_ffn_in['b2'], 'L0_ffn_wg': _L0_ffn_in['wg'], 'L0_ffn_bg': _L0_ffn_in['bg'], 'L0_ffn_w3': _L0_ffn_in['w3'], 'L0_ffn_b3': _L0_ffn_in['b3']}

def reference(x, L0_tok_weight, L0_attn_Wq, L0_attn_Wk, L0_attn_Wv, L0_attn_Wo, L0_attn_bo, L0_ffn_gate_w, L0_ffn_gate_b, L0_ffn_w1, L0_ffn_b1, L0_ffn_w2, L0_ffn_b2, L0_ffn_wg, L0_ffn_bg, L0_ffn_w3, L0_ffn_b3):
    import jax
    import jax.numpy as jnp

    def _L0_tok_ref(image, weight):
        import jax, jax.numpy as jnp
        import numpy as np
        HIDDEN = 256
        PATCH = 16
        CHANNELS = 3
        PATCH_NDIM = CHANNELS * PATCH * PATCH
        INIT_STD = 1.0 / HIDDEN ** 0.5
        SCALE = 1.0 / (INIT_STD * PATCH_NDIM ** 0.5)
        B, H, W, C = image.shape
        P, Q = (H // PATCH, W // PATCH)
        x = image.reshape(B, P, PATCH, Q, PATCH, C)
        x = x.transpose(0, 1, 3, 2, 4, 5).reshape(B, P * Q, PATCH * PATCH * C)
        return SCALE * jnp.einsum('bnd,hd->bnh', x, weight)

    def _L0_attn_ref(x, Wq, Wk, Wv, Wo, bo):
        import jax, jax.numpy as jnp
        import numpy as np
        DIM = 256
        HEADS = 16
        DIM_HEAD = 64
        INNER = HEADS * DIM_HEAD
        SEQ = 1024
        BATCH = 1
        b, n, _ = x.shape
        beta = 1.0 / jnp.sqrt(jnp.float32(DIM_HEAD))

        def split_heads(t):
            return t.reshape(b, n, HEADS, DIM_HEAD).transpose(0, 2, 1, 3)
        q = split_heads(x @ Wq)
        k = split_heads(x @ Wk)
        v = split_heads(x @ Wv)
        scores = jnp.einsum('bhid,bhjd->bhij', q * beta, k)
        mask_value = -jnp.finfo(scores.dtype).max
        causal = jnp.triu(jnp.ones((n, n), dtype=bool), k=1)
        scores = jnp.where(causal, mask_value, scores)
        attn = jax.nn.softmax(scores, axis=-1)
        out = jnp.einsum('bhij,bhjd->bhid', attn, v)
        out = out.transpose(0, 2, 1, 3).reshape(b, n, INNER)
        return out @ Wo + bo

    def _L0_ffn_ref(x, gate_w, gate_b, w1, b1, w2, b2, wg, bg, w3, b3):
        import jax, jax.numpy as jnp
        import numpy as np
        B, S, H = (2, 256, 256)
        DFF = 512
        E = 8
        TOPK = 2

        def _expert_ffn(x, w1, b1, w2, b2, wg, bg, w3, b3):
            x1 = jnp.einsum('bsh,hf->bsf', x, w1) + b1
            x2 = jnp.einsum('bsh,hf->bsf', x, w2) + b2
            z = x1 * x2
            s = jax.nn.silu(jnp.einsum('bsf,fg->bsg', z, wg) + bg)
            return jnp.einsum('bsg,gh->bsh', s, w3) + b3
        logits = jnp.einsum('bsh,he->bse', x, gate_w) + gate_b
        topv, topi = jax.lax.top_k(logits, TOPK)
        probs = jax.nn.softmax(topv, axis=-1)
        out = jnp.zeros_like(x)
        for e in range(E):
            we = jnp.sum(probs * (topi == e), axis=-1)
            y = _expert_ffn(x, w1[e], b1[e], w2[e], b2[e], wg[e], bg[e], w3[e], b3[e])
            out = out + we[..., None] * y
        return out
    h = _L0_tok_ref(x, L0_tok_weight)
    h = h + _L0_attn_ref(_layernorm(h, axis=-1), L0_attn_Wq, L0_attn_Wk, L0_attn_Wv, L0_attn_Wo, L0_attn_bo)
    h = h + _L0_ffn_ref(_layernorm(h, axis=-1), L0_ffn_gate_w, L0_ffn_gate_b, L0_ffn_w1, L0_ffn_b1, L0_ffn_w2, L0_ffn_b2, L0_ffn_wg, L0_ffn_bg, L0_ffn_w3, L0_ffn_b3)
    return h

_drawn_inputs = setup_inputs


def setup_inputs(seed=0):
    import zlib

    import numpy as np

    out = dict(_drawn_inputs(seed))
    spreads = {'L0_ffn_gate_b': (0.0, 0.1),
     'L0_ffn_b1': (0.0, 0.8),
     'L0_ffn_b2': (0.0, 0.8),
     'L0_ffn_bg': (0.0, 1.501),
     'L0_ffn_b3': (0.0, 0.8)}
    factors = {'L0_attn_Wq': 6.696,
     'L0_attn_Wk': 6.868,
     'L0_ffn_w1': 7.22,
     'L0_ffn_w2': 7.216,
     'L0_ffn_wg': 6.89,
     'L0_ffn_w3': 3.075}
    for name, (base, spread) in spreads.items():
        noise = np.random.default_rng([zlib.crc32(name.encode()), seed]).standard_normal(out[name].shape)
        drawn = base * np.exp(spread * noise) if base else spread * noise
        out[name] = jnp.asarray(drawn.astype(out[name].dtype))
    for name, factor in factors.items():
        out[name] = (out[name] * factor).astype(out[name].dtype)
    return out
```

```python
import concourse.bass as bass
from concourse import mybir
from contextlib import ExitStack


def vit_block_kernel(
    nc: bass.Bass,
    patches: bass.AP,
    tok_w: bass.AP,
    wq: bass.AP,
    wk: bass.AP,
    wv: bass.AP,
    wo: bass.AP,
    bo: bass.AP,
    gate_w: bass.AP,
    gate_b: bass.AP,
    expert_w: bass.AP,
    expert_b: bass.AP,
    slot_rows: bass.AP,
    out: bass.AP,
):
    f32 = mybir.dt.float32
    f32r = mybir.dt.float32r
    bf16 = mybir.dt.bfloat16
    i32 = mybir.dt.int32
    u32 = mybir.dt.uint32
    ALU = mybir.AluOpType
    ACT = mybir.ActivationFunctionType
    AX = mybir.AxisListType

    P = 128
    TT, _, DC, _ = patches.shape
    TOK = TT * P
    H = tok_w.shape[1]
    HC = H // P
    INNER = wq.shape[1]
    DH = 64
    HEADS = INNER // DH
    IC = INNER // P
    SEQ = 16
    QUAD = 32
    NQ = P // QUAD
    E = gate_w.shape[1]
    TOPK = 2
    F = expert_b.shape[1] - H
    F //= 3
    FC = F // P
    EW = expert_w.shape[2]
    O_W1, O_W2, O_WG, O_W3 = 0, HC * F, 2 * HC * F, 2 * HC * F + FC * F
    O_B1, O_B2, O_BG, O_B3, EB = 0, F, 2 * F, 3 * F, 3 * F + H
    OVER = (TOK * TOPK - 1) // P
    BLOCKS = E + OVER
    ITERS = BLOCKS + 1
    EXTRA = ITERS + 2 - E
    SCALE = 1.0 / ((1.0 / H ** 0.5) * (DC * P) ** 0.5)
    EPS = 1e-5
    BETA = 1.0 / DH ** 0.5
    MASKED = -3.0e38
    CONSTS = 22

    ctx = ExitStack()
    with ctx:
        def sb(name, shape, dt=f32):
            return ctx.enter_context(nc.sbuf_tensor(name, shape, dt))

        def sem(name):
            return ctx.enter_context(nc.semaphore(name))

        early = sb("early", [P, DC * (TOK + H)])
        x_sb = early[:, 0:DC * TOK].rearrange("p (t c n) -> p t c n", t=TT, c=DC)
        tw_sb = early[:, DC * TOK:DC * (TOK + H)].rearrange("p (c h) -> p c h", c=DC)
        x2s, z, s = (early[:, a * F:(a + 1) * F] for a in range(3))
        zT, sT = (early[:, a * F:(a + 1) * F].rearrange("p (c n) -> p c n", c=FC) for a in (3, 4))
        ysb = early[:, 5 * F:5 * F + 2 * H].rearrange("p (a h) -> p a h", a=2)
        wq_sb = sb("wq_sb", [P, HC, INNER])
        wk_sb = sb("wk_sb", [P, HC, INNER])
        wv_sb = sb("wv_sb", [P, HC, INNER])
        wo_sb = sb("wo_sb", [P, IC, H])
        bo_sb = sb("bo_sb", [P, H])
        gw_sb = sb("gw_sb", [P, HC, E])
        gb_sb = sb("gb_sb", [P, E])
        ew = sb("ew", [P, 2, EW])
        braw = sb("braw", [P, EB])
        bparts = sb("bparts", [P, EB], f32r)
        hbuf = sb("hbuf", [P, TT, H])
        nrm = sb("nrm", [P, TT, H])
        stats = sb("stats", [P, TT, 6])
        mv = sb("mv", [P, TT, 2])
        std = sb("std", [P, TT])
        rstd = sb("rstd", [P, TT])
        nT = sb("nT", [P, HC, TOK])
        qT = sb("qT", [P, IC, TOK])
        kT = sb("kT", [P, IC, TOK])
        ysel = qT[:, 0:TOPK * TT * H // TOK, :].rearrange("p a n -> p (a n)").rearrange("p (k t h) -> p k t h", k=TOPK, t=TT)
        v_sb = sb("v_sb", [P, TT, INNER])
        mask = sb("mask", [P, QUAD])
        sc = sb("sc", [P, 2, HEADS, QUAD])
        mx = sb("mx", [P, 2, HEADS])
        rs = sb("rs", [P, 2, HEADS])
        rr = sb("rr", [P, 2, HEADS])
        pT = sb("pT", [P, 2, HEADS, QUAD])
        oT = sb("oT", [P, IC, TOK])
        ident = sb("ident", [P, P])
        lg = sb("lg", [P, TT, E])
        m8 = sb("m8", [P, TT, 8])
        ix8 = sb("ix8", [P, TT, 8], u32)
        ixf = sb("ixf", [P, TT, TOPK])
        iotai = sb("iotai", [P, P], i32)
        iota = sb("iota", [P, P])
        prowi = sb("prowi", [P, 1], i32)
        prow = sb("prow", [P, 2])
        lown = sb("lown", [P, 1])
        rowexp = sb("rowexp", [P, 1])
        pick = sb("pick", [P, TOPK, TT, E])
        both = sb("both", [P, TT, E], bf16)
        tri = sb("tri", [P, P], bf16)
        ones = sb("ones", [P, P], bf16)
        pos = sb("pos", [P, TT + 1, E])
        wk8 = sb("wk8", [P, 4, E])
        zero8 = sb("zero8", [P, E])
        cum = sb("cum", [P, E])
        obase = sb("obase", [P, E])
        slot8 = sb("slot8", [P, TT, E])
        over8 = sb("over8", [P, TT, E])
        pickslot = sb("pickslot", [P, TOPK, TT, E])
        slotf = sb("slotf", [P, TOPK, TT])
        sloti = sb("sloti", [P, TOPK, TT], u32)
        jle = sb("jle", [P, EXTRA, E])
        etab = sb("etab", [P, E + EXTRA])
        etabi = sb("etabi", [P, E + EXTRA], i32)
        nbf = sb("nbf", [P, 1])
        nbi = sb("nbi", [P, 1], i32)
        gdiff = sb("gdiff", [P, TT])
        gth = sb("gth", [P, TT])
        prob = sb("prob", [P, TOPK, TT])
        rel = sb("rel", [P, TOPK, TT])
        onehot = sb("onehot", [P, 2, TT, P])
        sel = sb("sel", [P, 2, P], f32r)
        sel3 = sb("sel3", [P, 2, P], f32r)
        eps_c = sb("eps_c", [P, 1])
        zrow = sb("zrow", [P, H])
        xT = sb("xT", [P, 2, HC, P])

        psA = ctx.enter_context(nc.psum_tensor("psA", [P, 2, 512], f32))
        psB = ctx.enter_context(nc.psum_tensor("psB", [P, 2, 512], f32))
        psC = ctx.enter_context(nc.psum_tensor("psC", [P, 4, 512], f32))
        p_x1, p_x2, p_gat, p_zT = psA[:, 0, :], psA[:, 1, :], psB[:, 0, 0:HC * P], psB[:, 1, :]
        p_g, p_sT, p_y = psC[:, 0, :], psC[:, 1, :], psC[:, 2, 0:H]

        x_loaded = [sem(f"x_loaded{t}") for t in range(TT)]
        tw_loaded, wv_loaded, wq_loaded, wk_loaded, wo_loaded, small_loaded, braw_loaded = (
            sem(n) for n in ("tw_loaded", "wv_loaded", "wq_loaded", "wk_loaded", "wo_loaded", "small_loaded", "braw_loaded"))
        w12_loaded, wg_loaded, w3_loaded = ([sem(f"{n}{i}") for i in range(2)] for n in ("w12_loaded", "wg_loaded", "w3_loaded"))
        const_ready = sem("const_ready")
        tok_done, h_ready, stats_done, var_ready, std_ready, rstd_ready, nrm_ready, nTp_done, nT_ready = (
            sem(n) for n in ("tok_done", "h_ready", "stats_done", "var_ready", "std_ready", "rstd_ready", "nrm_ready", "nTp_done", "nT_ready"))
        v_done, v_evac, q_done, q_evac, k_done, k_evac = (
            sem(n) for n in ("v_done", "v_evac", "q_done", "q_evac", "k_done", "k_evac"))
        sc_done, sc_evac, mx_ready, sub_ready, exp_ready, rs_ready, rr_ready, p_ready, pT_ready = (
            sem(n) for n in ("sc_done", "sc_evac", "mx_ready", "sub_ready", "exp_ready", "rs_ready", "rr_ready", "p_ready", "pT_ready"))
        pv_done, oT_ready, wo_done, hb_ready = (sem(n) for n in ("pv_done", "oT_ready", "wo_done", "hb_ready"))
        lg_done, lg_ready, m8_ready, ix_ready, pick_ready, both_ready, cum_done, route, table_ready = (
            sem(n) for n in ("lg_done", "lg_ready", "m8_ready", "ix_ready", "pick_ready", "both_ready", "cum_done", "route", "table_ready"))
        prob_step, gth_ready = sem("prob_step"), sem("gth_ready")
        sel3_ready, y_out_ready, h1_ready = sem("sel3_ready"), sem("y_out_ready"), sem("h1_ready")
        rel_ready, hot_part, hot_ready, sel_ready, gat_done, xT_ready, up_done, x2_ready, z_ready = (
            sem(n) for n in ("rel_ready", "hot_part", "hot_ready", "sel_ready", "gat_done", "xT_ready", "up_done", "x2_ready", "z_ready"))
        zTp_done, zT_ready, g_done, s_ready, sTp_done, sT_ready, y_done, y_ready = (
            sem(n) for n in ("zTp_done", "zT_ready", "g_done", "s_ready", "sTp_done", "sT_ready", "y_done", "y_ready"))
        y_stored = [sem(f"y_stored{i}") for i in range(2)]
        ysel_loaded = [sem(f"ysel_loaded{i}") for i in range(TT)]
        rows_zeroed = sem("rows_zeroed")
        mix_ready, out_ready, out_stored = sem("mix_ready"), sem("out_ready"), sem("out_stored")

        block = ctx.enter_context(nc.Block())


        def guarded(engine, n_blocks, block_no, stage, *args):
            if isinstance(block_no, int) and block_no < E:
                stage(block_no, *args)
            else:
                with engine.If(n_blocks > block_no):
                    stage(block_no, *args)

        @block.sync
        def _(sp):
            sp.dma_start(tw_sb[:], tok_w.rearrange("(c p) h -> p c h", p=P)).then_inc(tw_loaded, 16)
            for t in range(TT):
                sp.dma_start(x_sb[:, t], patches[t]).then_inc(x_loaded[t], 16)
            sp.dma_start(wv_sb[:], wv.rearrange("(c p) n -> p c n", p=P)).then_inc(wv_loaded, 16)
            sp.dma_start(wq_sb[:], wq.rearrange("(c p) n -> p c n", p=P)).then_inc(wq_loaded, 16)
            sp.dma_start(wk_sb[:], wk.rearrange("(c p) n -> p c n", p=P)).then_inc(wk_loaded, 16)
            sp.dma_start(wo_sb[:], wo.rearrange("(c p) n -> p c n", p=P)).then_inc(wo_loaded, 16)

            def load(ring, lo, hi, signal):
                def stage(b, par):
                    e = b if isinstance(b, int) else sp.value_load(etabi[0:1, bass.ds(b, 1)], min_val=0, max_val=E - 1)
                    sp.dma_start(ew[:, par, lo:hi], expert_w[bass.ds(e, 1), :, lo:hi].rearrange("e p n -> (e p) n")
                                 ).then_inc(signal[par], 16)
                return stage

            load_w12, load_wg, load_w3 = (load(ew, O_W1, O_WG, w12_loaded), load(ew, O_WG, O_W3, wg_loaded),
                                          load(ew, O_W3, EW, w3_loaded))
            for b in range(2):
                load_w12(b, b)
                load_wg(b, b)
                load_w3(b, b)
            sp.wait_ge(table_ready, 1)
            n_blocks = sp.value_load(nbi[0:1, 0:1], min_val=E, max_val=BLOCKS)

            def w12_behind_up(b, par):
                sp.wait_ge(up_done, b - 1)
                load_w12(b, par)

            def wg_behind_gate(b, par):
                sp.wait_ge(g_done, b - 1)
                load_wg(b, par)

            def w3_behind_down(b, par):
                sp.wait_ge(y_done, b - 1)
                load_w3(b, par)

            guarded(sp, n_blocks, 2, w12_behind_up, 0)
            guarded(sp, n_blocks, 3, w12_behind_up, 1)
            guarded(sp, n_blocks, 2, wg_behind_gate, 0)
            with sp.Fori(1, ITERS // 2) as i:
                for par in range(2):
                    k = 2 * i + par
                    guarded(sp, n_blocks, k + 2, w12_behind_up, par)
                    guarded(sp, n_blocks, k + 1, wg_behind_gate, 1 - par)
                    guarded(sp, n_blocks, k, w3_behind_down, par)
            for t in range(TT):
                sp.wait_ge(out_ready, t + 1)
                sp.dma_start(out[t * P:(t + 1) * P, :], hbuf[:, t]).then_inc(out_stored, 16)
            sp.wait_ge(out_stored, 16 * TT)

        @block.gpsimd
        def _(pool):
            nc.gpsimd.memset(ident[:], 0.0).then_inc(const_ready, 1)
            nc.gpsimd.memset(tri[:], 1.0).then_inc(const_ready, 1)
            nc.gpsimd.memset(ones[:], 1.0).then_inc(const_ready, 1)
            nc.gpsimd.memset(mask[:], 0.0).then_inc(const_ready, 1)
            nc.gpsimd.memset(zero8[:], 0.0).then_inc(const_ready, 1)
            nc.gpsimd.iota(iotai[:], pattern=[[1, P]], base=0, channel_multiplier=0).then_inc(const_ready, 1)
            nc.gpsimd.iota(prowi[:], pattern=[[0, 1]], base=0, channel_multiplier=1).then_inc(const_ready, 1)
            nc.gpsimd.memset(braw[:], 0.0).then_inc(const_ready, 1)
            nc.gpsimd.memset(eps_c[:], EPS).then_inc(const_ready, 1)
            nc.gpsimd.memset(zrow[:], 0.0).then_inc(const_ready, 1)
            pool.wait_ge(const_ready, 10)
            nc.gpsimd.affine_select(out=ident[:], in_=ident[:], compare_op=ALU.not_equal, fill=1.0, base=0,
                                    pattern=[[-1, P]], channel_multiplier=1).then_inc(const_ready, 1)
            pool.wait_ge(const_ready, 11)
            nc.gpsimd.affine_select(out=tri[:], in_=tri[:], compare_op=ALU.is_gt, fill=0.0, base=0,
                                    pattern=[[1, P]], channel_multiplier=-1).then_inc(const_ready, 1)
            for q in range(NQ):
                m = mask[q * QUAD:(q + 1) * QUAD, :]
                pool.wait_ge(const_ready, 12 + q)
                nc.gpsimd.affine_select(out=m, in_=m, compare_op=ALU.is_ge, fill=MASKED, base=0,
                                        pattern=[[-1, QUAD]], channel_multiplier=1).then_inc(const_ready, 1)
            for q in range(NQ):
                m = mask[q * QUAD:(q + 1) * QUAD, 0:SEQ]
                pool.wait_ge(const_ready, 16 + q)
                nc.gpsimd.affine_select(out=m, in_=m, compare_op=ALU.is_gt, fill=MASKED, base=SEQ,
                                        pattern=[[0, SEQ]], channel_multiplier=-1).then_inc(const_ready, 1)
            pool.wait_ge(const_ready, 20)
            nc.gpsimd.tensor_copy(iota[:], iotai[:]).then_inc(const_ready, 1)
            pool.wait_ge(const_ready, 21)
            nc.gpsimd.tensor_copy(prow[:, 0:1], prowi[:]).then_inc(const_ready, 1)
            pool.wait_ge(table_ready, 1)
            n_blocks = pool.value_load(nbi[0:1, 0:1], min_val=E, max_val=BLOCKS)

            def stored(b):
                pool.wait_ge(y_stored[b % 2], 16 * (b // 2 + 1))

            for b in range(E - 2, BLOCKS):
                guarded(pool, n_blocks, b, stored)
            for t in range(TT):
                for k in range(TOPK):
                    nc.gpsimd.indirect_dma_start(
                        out=ysel[:, k, t, :], out_offset=None, in_=slot_rows,
                        in_offset=bass.IndirectOffsetOnAxis(ap=sloti[:, k, t:t + 1], axis=0),
                        bounds_check=BLOCKS * P - 1, oob_is_err=True).then_inc(ysel_loaded[t], 16)

        @block.scalar
        def _(act):
            act.dma_start(bo_sb[:], bo.partition_broadcast(P)).then_inc(small_loaded, 16)
            act.dma_start(gw_sb[:], gate_w.rearrange("(c p) e -> p c e", p=P)).then_inc(small_loaded, 16)
            act.dma_start(gb_sb[:], gate_b.partition_broadcast(P)).then_inc(small_loaded, 16)
            act.wait_ge(const_ready, CONSTS)
            act.dma_start(slot_rows[E * P:BLOCKS * P, :].rearrange("(b p) h -> p b h", p=P),
                          zrow[:].rearrange("p (a h) -> p a h", a=1).broadcast_to([P, OVER, H])).then_inc(rows_zeroed, 16)
            act.dma_start(braw[0:E], expert_b).then_inc(braw_loaded, 16)
            act.dma_start(braw[E:2 * E], expert_b).then_inc(braw_loaded, 16)

            def deviation(n):
                act.wait_ge(var_ready, n + 1)
                t = n % TT
                nc.scalar.activation(std[:, t:t + 1], mv[:, t, 1:2], ACT.Sqrt, bias=eps_c[:]).then_inc(std_ready, 1)

            def transposed_out(n):
                act.wait_ge(nTp_done, n + 1)
                t = n % TT
                nc.scalar.activation(nT[:, :, t * P:(t + 1) * P], psB[:, t % 2, 0:HC * P].rearrange("p (c n) -> p c n", c=HC),
                                     ACT.Copy).then_inc(nT_ready, 1)

            for t in range(TT):
                act.wait_ge(tok_done, t + 1)
                nc.scalar.activation(hbuf[:, t], psA[:, t % 2, 0:H], ACT.Copy, scale=SCALE).then_inc(h_ready, 1)
                deviation(t)
            for t in range(TT):
                transposed_out(t)
            for c in range(IC):
                act.wait_ge(q_done, c + 1)
                nc.scalar.activation(qT[:, c], psC[:, 2 * (c % 2), :], ACT.Copy, scale=BETA).then_inc(q_evac, 1)

            def exponentials(t):
                act.wait_ge(sub_ready, t + 1)
                nc.scalar.activation(sc[:, t % 2], sc[:, t % 2], ACT.Exp).then_inc(exp_ready, 1)

            def heads_out(t):
                act.wait_ge(pv_done, t + 1)
                nc.scalar.activation(oT[:, :, t * P:(t + 1) * P].rearrange("p c (j q) -> p c j q", j=NQ),
                                     psC[:, :, 0:IC * QUAD].rearrange("p j (c q) -> p c j q", c=IC),
                                     ACT.Copy).then_inc(oT_ready, 1)

            exponentials(0)
            for t in range(1, TT):
                exponentials(t)
                heads_out(t - 1)
            heads_out(TT - 1)
            for t in range(TT):
                deviation(TT + t)
            for t in range(TT):
                transposed_out(TT + t)
            act.wait_ge(prob_step, 1)
            nc.scalar.activation(gth[:], gdiff[:], ACT.Tanh, scale=0.5).then_inc(gth_ready, 1)
            act.wait_ge(table_ready, 1)
            n_blocks = act.value_load(nbi[0:1, 0:1], min_val=E, max_val=BLOCKS)

            def x_out(b, par):
                act.wait_ge(gat_done, b + 1)
                nc.scalar.activation(xT[:, par].rearrange("p c n -> p (c n)"), p_gat, ACT.Copy).then_inc(xT_ready, 1)

            def x2_out(b):
                act.wait_ge(up_done, b + 1)
                nc.scalar.activation(x2s[:], p_x2, ACT.Copy).then_inc(x2_ready, 1)

            def zT_out(b):
                act.wait_ge(zTp_done, b + 1)
                nc.scalar.activation(zT[:].rearrange("p c n -> p (c n)"), p_zT, ACT.Copy).then_inc(zT_ready, 1)

            def silu(b):
                act.wait_ge(g_done, b + 1)
                nc.scalar.activation(s[:], p_g, ACT.Silu).then_inc(s_ready, 1)

            def sT_out(b):
                act.wait_ge(sTp_done, b + 1)
                nc.scalar.activation(sT[:].rearrange("p c n -> p (c n)"), p_sT, ACT.Copy).then_inc(sT_ready, 1)

            def y_out(b, par, reused=True):
                act.wait_ge(y_done, b + 1)
                if reused:
                    act.wait_ge(y_stored[par], 8 * (b - par))
                nc.scalar.activation(ysb[:, par], p_y, ACT.Copy).then_inc(y_ready, 1)
                act.wait_ge(y_ready, b + 1)
                rows = b * P
                act.dma_start(slot_rows[bass.ds(rows, P), :], ysb[:, par]).then_inc(y_stored[par], 16)

            act.wait_ge(rows_zeroed, 16)
            x_out(0, 0)
            x2_out(0)
            x_out(1, 1)
            zT_out(0)
            x2_out(1)
            x_out(2, 0)
            silu(0)
            zT_out(1)
            for k in range(2, 4):
                x2_out(k)
                sT_out(k - 2)
                x_out(k + 1, 1 - k % 2)
                silu(k - 1)
                y_out(k - 2, k % 2, False)
                zT_out(k)
            with act.Fori(2, ITERS // 2) as i:
                for par in range(2):
                    k = 2 * i + par
                    guarded(act, n_blocks, k, x2_out)
                    guarded(act, n_blocks, k - 2, sT_out)
                    guarded(act, n_blocks, k + 1, x_out, 1 - par)
                    guarded(act, n_blocks, k - 1, silu)
                    guarded(act, n_blocks, k - 2, y_out, par)
                    guarded(act, n_blocks, k, zT_out)
            guarded(act, n_blocks, BLOCKS - 1, sT_out)
            guarded(act, n_blocks, BLOCKS - 1, y_out, (BLOCKS - 1) % 2)

        @block.vector
        def _(dve):
            def layer_norm(n, source_ready, source_count):
                t = n % TT
                dve.wait_ge(source_ready, source_count)
                nc.vector.bn_stats(stats[:, t], hbuf[:, t]).then_inc(stats_done, 1)
                dve.wait_ge(stats_done, n + 1)
                nc.vector.bn_aggr(mv[:, t], stats[:, t]).then_inc(var_ready, 1)

            def layer_norm_end(n):
                t = n % TT
                dve.wait_ge(std_ready, n + 1)
                nc.vector.reciprocal(rstd[:, t:t + 1], std[:, t:t + 1]).then_inc(rstd_ready, 1)
                dve.wait_ge(rstd_ready, n + 1)
                nc.vector.tensor_scalar(nrm[:, t], hbuf[:, t], mv[:, t, 0:1], rstd[:, t:t + 1], ALU.subtract, ALU.mult
                                        ).then_inc(nrm_ready, 1)

            for t in range(TT):
                layer_norm(t, h_ready, t + 1)
                layer_norm_end(t)
            dve.wait_ge(small_loaded, 48)
            for t in range(TT):
                nc.vector.tensor_tensor(hbuf[:, t], hbuf[:, t], bo_sb[:], ALU.add).then_inc(hb_ready, 1)
            for t in range(TT):
                dve.wait_ge(v_done, t + 1)
                nc.vector.tensor_copy(v_sb[:, t], psC[:, 2 * (t % 2):2 * (t % 2) + 2, :].rearrange("p a n -> p (a n)")
                                      ).then_inc(v_evac, 1)
            dve.wait_ge(braw_loaded, 32)
            dve.wait_ge(const_ready, CONSTS)
            nc.vector.tensor_scalar(lown[:], prow[:, 0:1], float(E), -1.0, ALU.is_ge, ALU.mult).then_inc(route, 1)
            nc.vector.tensor_copy(bparts[:], braw[:]).then_inc(route, 1)
            dve.wait_ge(route, 2)
            nc.vector.scalar_tensor_tensor(rowexp[:], lown[:], float(E), prow[:, 0:1], ALU.mult, ALU.add).then_inc(route, 1)
            nc.vector.scalar_tensor_tensor(bparts[:], bparts[:].bitcast(f32), lown[:], braw[:], ALU.mult, ALU.add
                                           ).then_inc(route, 1)
            for c in range(IC):
                dve.wait_ge(k_done, c + 1)
                nc.vector.tensor_copy(kT[:, c], psC[:, 2 * (c % 2) + 1, :]).then_inc(k_evac, 1)
            def scores_out(t):
                b = t % 2
                dve.wait_ge(sc_done, t + 1)
                if t >= 2:
                    dve.wait_ge(pT_ready, t - 1)
                nc.vector.tensor_tensor(sc[:, b].rearrange("p (u c) k -> p u c k", u=2),
                                        psB[:, :, 0:IC * QUAD].rearrange("p u (c k) -> p u c k", c=IC),
                                        mask[:].rearrange("p (a b k) -> p a b k", a=1, b=1).broadcast_to([P, 2, IC, QUAD]),
                                        ALU.add).then_inc(sc_evac, 1)
                dve.wait_ge(sc_evac, t + 1)
                nc.vector.tensor_reduce(mx[:, b], sc[:, b], AX.X, ALU.max).then_inc(mx_ready, 1)
                dve.wait_ge(mx_ready, t + 1)
                nc.vector.tensor_tensor(sc[:, b], sc[:, b], mx[:, b].rearrange("p (h a) -> p h a", a=1).broadcast_to([P, HEADS, QUAD]),
                                        ALU.subtract).then_inc(sub_ready, 1)

            def probabilities(t):
                b = t % 2
                dve.wait_ge(exp_ready, t + 1)
                nc.vector.tensor_reduce(rs[:, b], sc[:, b], AX.X, ALU.add).then_inc(rs_ready, 1)
                dve.wait_ge(rs_ready, t + 1)
                nc.vector.reciprocal(rr[:, b], rs[:, b]).then_inc(rr_ready, 1)
                dve.wait_ge(rr_ready, t + 1)
                nc.vector.tensor_tensor(sc[:, b], sc[:, b], rr[:, b].rearrange("p (h a) -> p h a", a=1).broadcast_to([P, HEADS, QUAD]),
                                        ALU.mult).then_inc(p_ready, 1)
                dve.wait_ge(p_ready, t + 1)
                if t >= 2:
                    dve.wait_ge(pv_done, t - 1)
                nc.vector.transpose(pT[:, b].rearrange("p h k -> p (h k)"), sc[:, b].rearrange("p h k -> p (h k)")
                                    ).then_inc(pT_ready, 1)

            def hidden_out(t):
                dve.wait_ge(wo_done, t + 1)
                if t == 0:
                    dve.wait_ge(hb_ready, TT)
                nc.vector.tensor_tensor(hbuf[:, t], psA[:, t % 2, 0:H], hbuf[:, t], ALU.add).then_inc(h1_ready, 1)
                layer_norm(TT + t, h1_ready, t + 1)

            scores_out(0)
            scores_out(1)
            probabilities(0)
            scores_out(2)
            probabilities(1)
            hidden_out(0)
            scores_out(3)
            probabilities(2)
            hidden_out(1)
            probabilities(3)
            hidden_out(2)
            hidden_out(3)
            for t in range(TT):
                layer_norm_end(TT + t)
            for t in range(TT):
                dve.wait_ge(lg_done, t + 1)
                nc.vector.tensor_tensor(lg[:, t], psC[:, t, 0:E], gb_sb[:], ALU.add).then_inc(lg_ready, 1)
                dve.wait_ge(lg_ready, t + 1)
                nc.vector.max(m8[:, t], lg[:, t]).then_inc(m8_ready, 1)
                dve.wait_ge(m8_ready, t + 1)
                nc.vector.max_index(ix8[:, t], m8[:, t], lg[:, t]).then_inc(ix_ready, 1)
                dve.wait_ge(ix_ready, 2 * t + 1)
                nc.vector.tensor_copy(ixf[:, t], ix8[:, t, 0:TOPK]).then_inc(ix_ready, 1)
                dve.wait_ge(ix_ready, 2 * t + 2)
                for k in range(TOPK):
                    nc.vector.tensor_scalar(pick[:, k, t], iota[:, 0:E], ixf[:, t, k:k + 1], None, ALU.is_equal
                                            ).then_inc(pick_ready, 1)
                dve.wait_ge(pick_ready, TOPK * (t + 1))
                nc.vector.tensor_tensor(both[:, t], pick[:, 0, t], pick[:, 1, t], ALU.add).then_inc(both_ready, 1)
            nc.vector.tensor_tensor(gdiff[:], m8[:, :, 0], m8[:, :, 1], ALU.subtract).then_inc(prob_step, 1)

            chain = [4]

            def step(instruction):
                chain[0] += 1
                instruction.then_inc(route, 1)
                dve.wait_ge(route, chain[0])

            dve.wait_ge(cum_done, 1)
            step(nc.vector.tensor_copy(pos[:].rearrange("p t e -> p (t e)"), psA[:, 0, 0:(TT + 1) * E]))
            count = pos[:, TT]
            step(nc.vector.tensor_scalar(wk8[:, 0], count, float(P), None, ALU.is_gt))
            step(nc.vector.scalar_tensor_tensor(wk8[:, 1], count, float(2 * P), wk8[:, 0], ALU.is_gt, ALU.add))
            step(nc.vector.scalar_tensor_tensor(wk8[:, 2], count, float(3 * P), wk8[:, 1], ALU.is_gt, ALU.add))
            step(nc.vector.tensor_tensor_scan(cum[:], wk8[:, 2], zero8[:], 0.0, ALU.add, ALU.add))
            step(nc.vector.tensor_scalar(nbf[:], cum[:, E - 1:E], float(E), None, ALU.add))
            nc.vector.tensor_copy(nbi[:], nbf[:]).then_inc(route, 1)
            chain[0] += 1
            step(nc.vector.tensor_tensor(jle[:], cum[:].rearrange("p (a e) -> p a e", a=1).broadcast_to([P, EXTRA, E]),
                                         iota[:, 0:EXTRA].rearrange("p (j a) -> p j a", a=1).broadcast_to([P, EXTRA, E]), ALU.is_le))
            nc.vector.tensor_copy(etab[:, 0:E], iota[:, 0:E]).then_inc(route, 1)
            chain[0] += 1
            step(nc.vector.tensor_reduce(etab[:, E:E + EXTRA], jle[:], AX.X, ALU.add))
            step(nc.vector.tensor_scalar(etab[:], etab[:], float(E - 1), None, ALU.min))
            nc.vector.tensor_copy(etabi[:], etab[:]).then_inc(route, 1)
            chain[0] += 1
            step(nc.vector.tensor_scalar(wk8[:, 0], iota[:, 0:E], float(P), None, ALU.mult))
            step(nc.vector.tensor_tensor(obase[:], cum[:], wk8[:, 2], ALU.subtract))
            step(nc.vector.tensor_scalar(obase[:], obase[:], float(P), float((E - 1) * P), ALU.mult, ALU.add))
            step(nc.vector.tensor_tensor(obase[:], obase[:], wk8[:, 0], ALU.subtract))
            step(nc.vector.tensor_scalar(over8[:], pos[:, 0:TT], float(P), None, ALU.is_ge))
            step(nc.vector.tensor_tensor(over8[:], over8[:], obase[:].rearrange("p (a e) -> p a e", a=1).broadcast_to([P, TT, E]), ALU.mult))
            step(nc.vector.tensor_tensor(slot8[:], pos[:, 0:TT], wk8[:, 0:1].broadcast_to([P, TT, E]), ALU.add))
            step(nc.vector.tensor_tensor(slot8[:], slot8[:], over8[:], ALU.add))
            for k in range(TOPK):
                step(nc.vector.tensor_tensor(pickslot[:, k], pick[:, k], slot8[:], ALU.mult))
            step(nc.vector.tensor_reduce(slotf[:], pickslot[:], AX.X, ALU.add))
            nc.vector.tensor_copy(rel[:], slotf[:]).then_inc(rel_ready, 1)
            nc.vector.tensor_copy(sloti[:], slotf[:]).then_inc(table_ready, 1)

            n_blocks = dve.value_load(nbi[0:1, 0:1], min_val=E, max_val=BLOCKS)

            def build_onehot(b, par):
                dve.wait_ge(rel_ready, b + 1)
                if not isinstance(b, int) or b >= 2:
                    dve.wait_ge(gat_done, b - 1)
                for t in range(TT):
                    nc.vector.tensor_scalar(onehot[:, par, t], iota[:], rel[:, 0, t:t + 1], None, ALU.is_equal
                                            ).then_inc(hot_part, 1)
                for t in range(TT):
                    dve.wait_ge(hot_part, TT * b + t + 1)
                    nc.vector.scalar_tensor_tensor(onehot[:, par, t], iota[:], rel[:, 1, t:t + 1], onehot[:, par, t],
                                                   ALU.is_equal, ALU.add).then_inc(hot_ready, 1)
                dve.wait_ge(hot_ready, TT * (b + 1))
                nc.vector.tensor_scalar(rel[:], rel[:], -float(P), None, ALU.add).then_inc(rel_ready, 1)

            def pick_biases(b, par, picker, ready):
                nc.vector.tensor_scalar(picker[:, par], etab[:, bass.ds(b, 1)].broadcast_to([P, P]), rowexp[:], None,
                                        ALU.is_equal).then_inc(ready, 1)

            def pick_up(b, par):
                if not isinstance(b, int) or b >= 2:
                    dve.wait_ge(g_done, b - 1)
                pick_biases(b, par, sel, sel_ready)

            def pick_down(b, par):
                if not isinstance(b, int) or b >= 2:
                    dve.wait_ge(y_done, b - 1)
                pick_biases(b, par, sel3, sel3_ready)

            def gated(b):
                dve.wait_ge(x2_ready, b + 1)
                if not isinstance(b, int) or b >= 1:
                    dve.wait_ge(zTp_done, b)
                nc.vector.tensor_tensor(z[:], p_x1, x2s[:], ALU.mult).then_inc(z_ready, 1)

            build_onehot(0, 0)
            pick_up(0, 0)
            build_onehot(1, 1)
            gated(0)
            build_onehot(2, 0)
            pick_up(1, 1)
            gated(1)
            build_onehot(3, 1)
            pick_down(0, 0)
            pick_up(2, 0)
            with dve.Fori(1, ITERS // 2) as i:
                for par in range(2):
                    k = 2 * i + par
                    guarded(dve, n_blocks, k, gated)
                    guarded(dve, n_blocks, k + 2, build_onehot, par)
                    guarded(dve, n_blocks, k - 1, pick_down, 1 - par)
                    guarded(dve, n_blocks, k + 1, pick_up, 1 - par)
            dve.wait_ge(gth_ready, 1)
            nc.vector.tensor_scalar(prob[:, 0], gth[:], 0.5, 0.5, ALU.mult, ALU.add).then_inc(prob_step, 1)
            nc.vector.tensor_scalar(prob[:, 1], gth[:], -0.5, 0.5, ALU.mult, ALU.add).then_inc(prob_step, 1)
            dve.wait_ge(prob_step, 3)
            for t in range(TT):
                dve.wait_ge(ysel_loaded[t], 16 * TOPK)
                nc.vector.scalar_tensor_tensor(hbuf[:, t], ysel[:, 0, t], prob[:, 0, t:t + 1], hbuf[:, t], ALU.mult, ALU.add
                                               ).then_inc(mix_ready, 1)
                dve.wait_ge(mix_ready, t + 1)
                nc.vector.scalar_tensor_tensor(hbuf[:, t], ysel[:, 1, t], prob[:, 1, t:t + 1], hbuf[:, t], ALU.mult, ALU.add
                                               ).then_inc(out_ready, 1)

        @block.tensor
        def _(pe):
            mm = nc.tensor.matmul
            pe.wait_ge(tw_loaded, 16)
            for t in range(TT):
                pe.wait_ge(x_loaded[t], 16)
                if t >= 2:
                    pe.wait_ge(h_ready, t - 1)
                for c in range(DC):
                    last = mm(psA[:, t % 2, 0:H], x_sb[:, t, c], tw_sb[:, c], start=(c == 0), stop=(c == DC - 1))
                last.then_inc(tok_done, 1)
            pe.wait_ge(const_ready, CONSTS)

            def transposes(n):
                t = n % TT
                pe.wait_ge(nrm_ready, n + 1)
                if n >= 2:
                    pe.wait_ge(nT_ready, n - 1)
                for c in range(HC):
                    last = nc.tensor.transpose(psB[:, t % 2, c * P:(c + 1) * P], nrm[:, t, c * P:(c + 1) * P], ident[:])
                last.then_inc(nTp_done, 1)

            def values(t):
                pe.wait_ge(nT_ready, t + 1)
                if t >= 2:
                    pe.wait_ge(v_evac, t - 1)
                for a in range(2):
                    for c in range(HC):
                        last = mm(psC[:, 2 * (t % 2) + a, :], nT[:, c, t * P:(t + 1) * P],
                                  wv_sb[:, c, a * 512:(a + 1) * 512], start=(c == 0), stop=(c == HC - 1))
                last.then_inc(v_done, 1)

            transposes(0)
            pe.wait_ge(wv_loaded, 16)
            for t in range(TT):
                if t + 1 < TT:
                    transposes(t + 1)
                values(t)

            def project(c, w, bank, done, evacuated):
                if c < 2:
                    pe.wait_ge(v_evac, TT - 1 + c)
                else:
                    pe.wait_ge(evacuated, c - 1)
                for a in range(HC):
                    last = mm(psC[:, bank, :], w[:, a, c * P:(c + 1) * P], nT[:, a, :], start=(a == 0), stop=(a == HC - 1))
                last.then_inc(done, 1)

            pe.wait_ge(wq_loaded, 16)
            pe.wait_ge(wk_loaded, 16)
            for c in range(IC):
                project(c, wq_sb, 2 * (c % 2), q_done, q_evac)
                project(c, wk_sb, 2 * (c % 2) + 1, k_done, k_evac)

            def scores(t):
                if t >= 1:
                    pe.wait_ge(sc_evac, t)
                for c in range(IC):
                    for j in range(NQ):
                        tok = slice(t * P + j * QUAD, t * P + (j + 1) * QUAD)
                        for u in range(2):
                            last = mm(psB[j * QUAD:(j + 1) * QUAD, u, c * QUAD:(c + 1) * QUAD],
                                      qT[u * DH:(u + 1) * DH, c, tok], kT[u * DH:(u + 1) * DH, c, tok], start=True, stop=True)
                last.then_inc(sc_done, 1)

            def weigh_values(t):
                pe.wait_ge(pT_ready, t + 1)
                if t >= 1:
                    pe.wait_ge(oT_ready, t)
                for c in range(IC):
                    for u in range(2):
                        for j in range(NQ):
                            quad = slice(j * QUAD, (j + 1) * QUAD)
                            last = mm(psC[u * DH:(u + 1) * DH, j, c * QUAD:(c + 1) * QUAD],
                                      v_sb[quad, t, (2 * c + u) * DH:(2 * c + u + 1) * DH], pT[quad, t % 2, u * IC + c, :],
                                      start=True, stop=True)
                last.then_inc(pv_done, 1)

            def project_out(t):
                pe.wait_ge(oT_ready, t + 1)
                if t >= 2:
                    pe.wait_ge(h1_ready, t - 1)
                for c in range(IC):
                    last = mm(psA[:, t % 2, 0:H], oT[:, c, t * P:(t + 1) * P], wo_sb[:, c], start=(c == 0), stop=(c == IC - 1))
                last.then_inc(wo_done, 1)

            pe.wait_ge(q_evac, IC)
            pe.wait_ge(k_evac, IC)
            scores(0)
            scores(1)
            pe.wait_ge(wo_loaded, 16)
            weigh_values(0)
            scores(2)
            project_out(0)
            weigh_values(1)
            scores(3)
            project_out(1)
            weigh_values(2)
            project_out(2)
            weigh_values(3)
            project_out(3)
            pe.wait_ge(sc_evac, TT)
            for t in range(TT):
                transposes(TT + t)
            pe.wait_ge(small_loaded, 48)
            for t in range(TT):
                pe.wait_ge(nT_ready, TT + t + 1)
                for c in range(HC):
                    last = mm(psC[:, t, 0:E], nT[:, c, t * P:(t + 1) * P], gw_sb[:, c], start=(c == 0), stop=(c == HC - 1))
                last.then_inc(lg_done, 1)
            for t in range(TT + 1):
                pe.wait_ge(both_ready, min(t + 1, TT))
                for a in range(min(t + 1, TT)):
                    last = mm(psA[:, 0, t * E:(t + 1) * E], tri[:] if a == t else ones[:], both[:, a],
                              start=(a == 0), stop=(a == min(t, TT - 1)))
            last.then_inc(cum_done, 1)
            pe.wait_ge(table_ready, 1)
            n_blocks = pe.value_load(nbi[0:1, 0:1], min_val=E, max_val=BLOCKS)

            def gather(b, par):
                pe.wait_ge(hot_ready, TT * (b + 1))
                if not isinstance(b, int) or b >= 1:
                    pe.wait_ge(xT_ready, b)
                for c in range(HC):
                    for t in range(TT):
                        last = mm(p_gat[:, c * P:(c + 1) * P], nrm[:, t, c * P:(c + 1) * P], onehot[:, par, t],
                                  start=(t == 0), stop=(t == TT - 1))
                last.then_inc(gat_done, 1)

            def up(b, par):
                pe.wait_ge(xT_ready, b + 1)
                pe.wait_ge(sel_ready, b + 1)
                pe.wait_ge(w12_loaded[par], 8 * (b - par) + 16)
                if not isinstance(b, int) or b >= 1:
                    pe.wait_ge(z_ready, b)
                for bank, ob, ow in ((p_x1, O_B1, O_W1), (p_x2, O_B2, O_W2)):
                    mm(bank, sel[:, par], bparts[:, ob:ob + F], start=True, stop=False)
                    for c in range(HC):
                        last = mm(bank, xT[:, par, c], ew[:, par, ow + c * F:ow + (c + 1) * F], start=False, stop=(c == HC - 1))
                last.then_inc(up_done, 1)

            def transpose_z(b):
                pe.wait_ge(z_ready, b + 1)
                if not isinstance(b, int) or b >= 1:
                    pe.wait_ge(zT_ready, b)
                for c in range(FC):
                    last = nc.tensor.transpose(p_zT[:, c * P:(c + 1) * P], z[:, c * P:(c + 1) * P], ident[:])
                last.then_inc(zTp_done, 1)

            def gate(b, par):
                pe.wait_ge(zT_ready, b + 1)
                pe.wait_ge(wg_loaded[par], 8 * (b - par) + 16)
                if not isinstance(b, int) or b >= 1:
                    pe.wait_ge(s_ready, b)
                mm(p_g, sel[:, par], bparts[:, O_BG:O_BG + F], start=True, stop=False)
                for c in range(FC):
                    last = mm(p_g, zT[:, c], ew[:, par, O_WG + c * F:O_WG + (c + 1) * F], start=False, stop=(c == FC - 1))
                last.then_inc(g_done, 1)

            def transpose_s(b):
                pe.wait_ge(s_ready, b + 1)
                if not isinstance(b, int) or b >= 1:
                    pe.wait_ge(sT_ready, b)
                for c in range(FC):
                    last = nc.tensor.transpose(p_sT[:, c * P:(c + 1) * P], s[:, c * P:(c + 1) * P], ident[:])
                last.then_inc(sTp_done, 1)

            def down(b, par):
                pe.wait_ge(sT_ready, b + 1)
                pe.wait_ge(sel3_ready, b + 1)
                pe.wait_ge(w3_loaded[par], 8 * (b - par) + 16)
                if not isinstance(b, int) or b >= 1:
                    pe.wait_ge(y_ready, b)
                mm(p_y, sel3[:, par], bparts[:, O_B3:O_B3 + H], start=True, stop=False)
                for c in range(FC):
                    last = mm(p_y, sT[:, c], ew[:, par, O_W3 + c * H:O_W3 + (c + 1) * H], start=False, stop=(c == FC - 1))
                last.then_inc(y_done, 1)

            gather(0, 0)
            up(0, 0)
            gather(1, 1)
            transpose_z(0)
            up(1, 1)
            gather(2, 0)
            gate(0, 0)
            transpose_z(1)
            with pe.Fori(1, ITERS // 2) as i:
                for par in range(2):
                    k = 2 * i + par
                    guarded(pe, n_blocks, k, up, par)
                    guarded(pe, n_blocks, k - 2, transpose_s)
                    guarded(pe, n_blocks, k + 1, gather, 1 - par)
                    guarded(pe, n_blocks, k - 1, gate, 1 - par)
                    guarded(pe, n_blocks, k - 2, down, par)
                    guarded(pe, n_blocks, k, transpose_z)
            guarded(pe, n_blocks, BLOCKS - 1, transpose_s)
            guarded(pe, n_blocks, BLOCKS - 1, down, (BLOCKS - 1) % 2)


def kernel(**inputs):
    import numpy as _np
    import concourse.bacc as _bacc
    from concourse import mybir as _mybir
    from concourse.bass_utils import run_bass_kernel_spmd as _run

    P, PATCH = 128, 16
    x = _np.asarray(inputs["x"])
    n, height, width, chans = x.shape
    rows, cols = height // PATCH, width // PATCH
    pt = x.reshape(n, rows, PATCH, cols, PATCH, chans).transpose(0, 1, 3, 2, 4, 5).reshape(n * rows * cols, -1)
    tokens, d = pt.shape
    pt = pt.reshape(tokens // P, P, d // P, P).transpose(0, 3, 2, 1)
    e, h, f = inputs["L0_ffn_w1"].shape

    def chunks(w):
        w = _np.asarray(w)
        return w.reshape(e, w.shape[1] // P, P, w.shape[2]).transpose(0, 2, 1, 3).reshape(e, P, -1)

    laid = {
        "patches": pt,
        "tok_w": _np.asarray(inputs["L0_tok_weight"]).T,
        "wq": inputs["L0_attn_Wq"], "wk": inputs["L0_attn_Wk"], "wv": inputs["L0_attn_Wv"],
        "wo": inputs["L0_attn_Wo"], "bo": inputs["L0_attn_bo"],
        "gate_w": inputs["L0_ffn_gate_w"], "gate_b": inputs["L0_ffn_gate_b"],
        "expert_w": _np.concatenate([chunks(inputs["L0_ffn_" + k]) for k in ("w1", "w2", "wg", "w3")], axis=2),
        "expert_b": _np.concatenate([_np.asarray(inputs["L0_ffn_" + k]) for k in ("b1", "b2", "bg", "b3")], axis=1),
    }
    nc = _bacc.Bacc("TRN2", target_bir_lowering=False, num_devices=1)
    arrays, args = {}, []
    for name, a in laid.items():
        a = _np.ascontiguousarray(a)
        arrays[f"in_{name}"] = a
        args.append(nc.dram_tensor(f"in_{name}", a.shape, _mybir.dt.from_np(a.dtype), kind="ExternalInput").ap())
    blocks = e + (2 * tokens - 1) // P
    args.append(nc.dram_tensor("slot_rows", (blocks * P, h), _mybir.dt.float32, kind="Internal").ap())
    args.append(nc.dram_tensor("out_0", (tokens, h), _mybir.dt.float32, kind="ExternalOutput").ap())
    vit_block_kernel(nc, *args)
    r = _run(nc, [arrays], core_ids=[0])
    return r.results[0]["out_0"].reshape(n, rows * cols, h)
```

```python
import concourse.bass as bass
from concourse import mybir
from contextlib import ExitStack


def vit_block_kernel(
    nc: bass.Bass,
    patches: bass.AP,
    tok_w: bass.AP,
    wq: bass.AP,
    wk: bass.AP,
    wv: bass.AP,
    wo: bass.AP,
    bo: bass.AP,
    gate_w: bass.AP,
    gate_b: bass.AP,
    expert_w: bass.AP,
    b3: bass.AP,
    slot_rows: bass.AP,
    out: bass.AP,
    ffn: int,
):
    f32 = mybir.dt.float32
    f32r = mybir.dt.float32r
    bf16 = mybir.dt.bfloat16
    i32 = mybir.dt.int32
    u32 = mybir.dt.uint32
    ALU = mybir.AluOpType
    ACT = mybir.ActivationFunctionType
    AX = mybir.AxisListType

    P = 128
    TT, _, DC, _ = patches.shape
    TOK = TT * P
    H = tok_w.shape[1]
    HC = H // P
    INNER = wq.shape[1]
    DH = 64
    HEADS = INNER // DH
    IC = INNER // P
    SEQ = 16
    QUAD = 32
    NQ = P // QUAD
    E = gate_w.shape[1]
    TOPK = 2
    FC = ffn // P
    F = ffn
    EW = expert_w.shape[2]
    O_W1, O_W2, O_WG = 0, HC * F, 2 * HC * F
    O_B1 = O_WG + FC * F
    O_B2 = O_B1 + FC
    O_W3 = O_B2 + FC
    O_BG = O_W3 + FC * H
    OVER = (TOK * TOPK - 1) // P
    BLOCKS = E + OVER
    ITERS = BLOCKS + 1
    EXTRA = ITERS + 2 - E
    SCALE = 1.0 / ((1.0 / H ** 0.5) * (DC * P) ** 0.5)
    EPS = 1e-5
    BETA = 1.0 / DH ** 0.5
    MASKED = -3.0e38
    CONSTS = 21

    ctx = ExitStack()
    with ctx:
        def sb(name, shape, dt=f32):
            return ctx.enter_context(nc.sbuf_tensor(name, shape, dt))

        def sem(name):
            return ctx.enter_context(nc.semaphore(name))

        early = sb("early", [P, DC * (TOK + H)])
        x_sb = early[:, 0:DC * TOK].rearrange("p (t c n) -> p t c n", t=TT, c=DC)
        tw_sb = early[:, DC * TOK:DC * (TOK + H)].rearrange("p (c h) -> p c h", c=DC)
        x2s = early[:, 0:F].rearrange("p (c n) -> p c n", c=FC)
        zT, sT = (early[:, a * F:(a + 2) * F].rearrange("p (b c n) -> p b c n", b=2, c=FC) for a in (1, 3))
        o_tok = early[:, 0:2 * INNER].rearrange("p (a n) -> p a n", a=2)
        ysb = early[:, 5 * F:5 * F + 2 * H].rearrange("p (a h) -> p a h", a=2)
        wq_sb = sb("wq_sb", [P, HC, INNER])
        wk_sb = sb("wk_sb", [P, HC, INNER])
        wv_sb = sb("wv_sb", [P, HC, INNER])
        wo_sb = sb("wo_sb", [P, IC, H])
        qT = sb("qT", [P, IC, TOK])
        kT = sb("kT", [P, IC, TOK])
        v_sb = sb("v_sb", [P, TT, INNER])
        oT = sb("oT", [P, IC, TOK])
        ysel = qT[:, 0:TOPK * TT * H // TOK, :].rearrange("p a n -> p (a n)").rearrange("p (k t h) -> p k t h", k=TOPK, t=TT)
        bo_sb = sb("bo_sb", [P, H])
        gw_sb = sb("gw_sb", [P, HC, E])
        gb_sb = sb("gb_sb", [P, E])
        ew = sb("ew", [P, 2, EW])
        b3_sb = sb("b3_sb", [P, 2, H])
        hbuf = sb("hbuf", [P, TT, H])
        nrm = sb("nrm", [P, TT, H])
        stats = sb("stats", [P, TT, 6])
        mv = sb("mv", [P, TT, 2])
        lnv = sb("lnv", [P, TT])
        rough = sb("rough", [P, TT])
        newton = sb("newton", [P, TT, 2])
        rstd = sb("rstd", [P, TT])
        nT = sb("nT", [P, HC, TOK])
        mask = sb("mask", [P, QUAD])
        sc = sb("sc", [P, 2, HEADS, QUAD])
        mx = sb("mx", [P, 2, HEADS])
        rs = sb("rs", [P, 2, HEADS])
        rr = sb("rr", [P, 2, HEADS])
        pT = sb("pT", [P, 2, HEADS, QUAD])
        ident = sb("ident", [P, P])
        lg = sb("lg", [P, TT, E])
        m8 = sb("m8", [P, TT, 8])
        ix8 = sb("ix8", [P, TT, 8], u32)
        ixf = sb("ixf", [P, TOPK, TT])
        iotai = sb("iotai", [P, P], i32)
        iota = sb("iota", [P, P])
        prowi = sb("prowi", [P, 1], i32)
        prow = sb("prow", [P, 2])
        pick = sb("pick", [P, TOPK, TT, E])
        both = sb("both", [P, TT, E], bf16)
        absent = sb("absent", [P, TT, E])
        tri = sb("tri", [P, P], bf16)
        ones = sb("ones", [P, P], bf16)
        pos = sb("pos", [P, TT + 1, E])
        wk8 = sb("wk8", [P, 4, E])
        zero8 = sb("zero8", [P, E])
        cum = sb("cum", [P, E])
        sbase = sb("sbase", [P, E])
        obase = sb("obase", [P, E])
        slot8 = sb("slot8", [P, TT, E])
        over8 = sb("over8", [P, TT, E])
        pickslot = sb("pickslot", [P, TOPK, TT, E])
        slotf = sb("slotf", [P, TOPK, TT])
        sloti = sb("sloti", [P, TOPK, TT], u32)
        jle = sb("jle", [P, EXTRA, E])
        etab = sb("etab", [P, E + EXTRA])
        etabi = sb("etabi", [P, E + EXTRA], i32)
        nbf = sb("nbf", [P, 1])
        nbi = sb("nbi", [P, 1], i32)
        gdiff = sb("gdiff", [P, TT])
        gth = sb("gth", [P, TT])
        prob = sb("prob", [P, TOPK, TT])
        rank = sb("rank", [P, TT, E])
        rank_b = sb("rank_b", [P, 2, TT])
        nrm_parts = sb("nrm_parts", [P, 2, TT, H], f32r)
        rel = sb("rel", [P, TOPK, TT])
        onehot = sb("onehot", [P, TT, 2 * P], f32r)
        eps_c = sb("eps_c", [P, 1])
        zrow = sb("zrow", [P, H])
        xT = sb("xT", [P, HC, 2 * P])

        psA = ctx.enter_context(nc.psum_tensor("psA", [P, 2, 512], f32))
        psB = ctx.enter_context(nc.psum_tensor("psB", [P, 2, 512], f32))
        psC = ctx.enter_context(nc.psum_tensor("psC", [P, 4, 512], f32))
        p_x1, p_x2, p_gat, p_g, p_y = psA[:, 0, :], psA[:, 1, :], psB[:, 0, :], psB[:, 1, :], psC[:, 0, 0:H]

        x_loaded = [sem(f"x_loaded{t}") for t in range(TT)]
        tw_loaded, wv_loaded, wq_loaded, wk_loaded, wo_loaded, small_loaded = (
            sem(n) for n in ("tw_loaded", "wv_loaded", "wq_loaded", "wk_loaded", "wo_loaded", "small_loaded"))
        w12_loaded, wg_loaded, w3_loaded = ([sem(f"{n}{i}") for i in range(2)] for n in ("w12_loaded", "wg_loaded", "w3_loaded"))
        const_ready = sem("const_ready")
        tok_done, h_ready, stats_done, var_ready, ln_ready, rough_ready, newton_ready, rstd_ready, nrm_ready, nTp_done, nT_ready = (
            sem(n) for n in ("tok_done", "h_ready", "stats_done", "var_ready", "ln_ready", "rough_ready", "newton_ready", "rstd_ready", "nrm_ready", "nTp_done", "nT_ready"))
        v_done, v_evac, q_done, q_evac, k_done, k_evac = (
            sem(n) for n in ("v_done", "v_evac", "q_done", "q_evac", "k_done", "k_evac"))
        sc_done, sc_evac, mx_ready, sub_ready, exp_ready, rs_ready, rr_ready, p_ready, pT_ready = (
            sem(n) for n in ("sc_done", "sc_evac", "mx_ready", "sub_ready", "exp_ready", "rs_ready", "rr_ready", "p_ready", "pT_ready"))
        pv_done, o_ready, oTp_done, oT_ready, wo_done, hb_ready = (
            sem(n) for n in ("pv_done", "o_ready", "oTp_done", "oT_ready", "wo_done", "hb_ready"))
        lg_done, lg_ready, m8_ready, ix_ready, pick_ready, both_ready, absent_ready, cum_done, route, table_ready, slots_ready = (
            sem(n) for n in ("lg_done", "lg_ready", "m8_ready", "ix_ready", "pick_ready", "both_ready", "absent_ready", "cum_done", "route", "table_ready", "slots_ready"))
        prob_step, gth_ready = sem("prob_step"), sem("gth_ready")
        h1_ready, ixf_ready = sem("h1_ready"), sem("ixf_ready")
        rel_ready, hot_part, hot_ready, gat_done, xT_ready, up_done, x2_ready, z_ready = (
            sem(n) for n in ("rel_ready", "hot_part", "hot_ready", "gat_done", "xT_ready", "up_done", "x2_ready", "z_ready"))
        g_done, s_ready, y_done, y_ready, rank_ready, nh_ready, nl_ready = (
            sem(n) for n in ("g_done", "s_ready", "y_done", "y_ready", "rank_ready", "nh_ready", "nl_ready"))
        y_stored = [sem(f"y_stored{i}") for i in range(2)]
        ysel_loaded = [sem(f"ysel_loaded{i}") for i in range(TT)]
        rows_zeroed = sem("rows_zeroed")
        rel_renewed = sem("rel_renewed")
        mix_ready, out_ready, out_stored = sem("mix_ready"), sem("out_ready"), sem("out_stored")

        block = ctx.enter_context(nc.Block())

        def fixed(b):
            return isinstance(b, int)

        def at_least(engine, signal, count):
            if not fixed(count) or count >= 1:
                engine.wait_ge(signal, count)


        def guarded(engine, n_blocks, block_no, stage, *args):
            if fixed(block_no) and block_no < E:
                if block_no >= 0:
                    stage(block_no, *args)
            else:
                with engine.If(n_blocks > block_no):
                    stage(block_no, *args)

        @block.sync
        def _(sp):
            sp.dma_start(tw_sb[:], tok_w.rearrange("(c p) h -> p c h", p=P)).then_inc(tw_loaded, 16)
            for t in range(TT):
                sp.dma_start(x_sb[:, t], patches[t]).then_inc(x_loaded[t], 16)
            sp.dma_start(wv_sb[:], wv.rearrange("(c p) n -> p c n", p=P)).then_inc(wv_loaded, 16)
            sp.dma_start(wq_sb[:], wq.rearrange("(c p) n -> p c n", p=P)).then_inc(wq_loaded, 16)
            sp.dma_start(wk_sb[:], wk.rearrange("(c p) n -> p c n", p=P)).then_inc(wk_loaded, 16)
            sp.dma_start(wo_sb[:], wo.rearrange("(c p) n -> p c n", p=P)).then_inc(wo_loaded, 16)

            def expert(b):
                return b if fixed(b) else sp.value_load(etabi[0:1, bass.ds(b, 1)], min_val=0, max_val=E - 1)

            def load(e, par, lo, hi, signal):
                sp.dma_start(ew[:, par, lo:hi], expert_w[bass.ds(e, 1), :, lo:hi].rearrange("e p n -> (e p) n")
                             ).then_inc(signal[par], 16)

            def load_w12(b, par):
                load(expert(b), par, 0, O_WG, w12_loaded)

            def load_wg(b, par):
                load(expert(b), par, O_WG, O_W3, wg_loaded)

            def load_w3(b, par):
                e = expert(b)
                load(e, par, O_W3, EW, w3_loaded)
                sp.dma_start(b3_sb[:, par], b3[bass.ds(e, 1), :].rearrange("e h -> (e h)").partition_broadcast(P)
                             ).then_inc(w3_loaded[par], 16)

            for b in range(2):
                load_w12(b, b)
                load_wg(b, b)
                load_w3(b, b)

            def next_w12(b, par):
                sp.wait_ge(up_done, b - 1)
                load_w12(b, par)

            def next_wg(b, par):
                sp.wait_ge(g_done, b - 1)
                load_wg(b, par)

            def next_w3(b, par):
                sp.wait_ge(y_ready, b - 1)
                load_w3(b, par)

            def store_y(b, par):
                sp.wait_ge(y_ready, b + 1)
                sp.dma_start(slot_rows[bass.ds(b * P, P), :], ysb[:, par]).then_inc(y_stored[par], 16)

            sp.wait_ge(rows_zeroed, 16)

            def turn(k, par, n_blocks=None):
                guarded(sp, n_blocks, k + 2, next_w12, par)
                if not fixed(k) or k >= 1:
                    guarded(sp, n_blocks, k + 1, next_wg, 1 - par)
                guarded(sp, n_blocks, k - 2, store_y, par)
                if not fixed(k) or k >= 2:
                    guarded(sp, n_blocks, k, next_w3, par)

            for k in range(4):
                turn(k, k % 2)
            sp.wait_ge(table_ready, 1)
            n_blocks = sp.value_load(nbi[0:1, 0:1], min_val=E, max_val=BLOCKS)
            with sp.Fori(2, ITERS // 2) as i:
                for par in range(2):
                    turn(2 * i + par, par, n_blocks)
            guarded(sp, n_blocks, BLOCKS - 1, store_y, (BLOCKS - 1) % 2)
            for t in range(TT):
                sp.wait_ge(out_ready, t + 1)
                sp.dma_start(out[t * P:(t + 1) * P, :], hbuf[:, t]).then_inc(out_stored, 16)
            sp.wait_ge(out_stored, 16 * TT)

        @block.gpsimd
        def _(pool):
            nc.gpsimd.memset(ident[:], 0.0).then_inc(const_ready, 1)
            nc.gpsimd.memset(tri[:], 1.0).then_inc(const_ready, 1)
            nc.gpsimd.memset(ones[:], 1.0).then_inc(const_ready, 1)
            nc.gpsimd.memset(mask[:], 0.0).then_inc(const_ready, 1)
            nc.gpsimd.memset(zero8[:], 0.0).then_inc(const_ready, 1)
            nc.gpsimd.iota(iotai[:], pattern=[[1, P]], base=0, channel_multiplier=0).then_inc(const_ready, 1)
            nc.gpsimd.iota(prowi[:], pattern=[[0, 1]], base=0, channel_multiplier=1).then_inc(const_ready, 1)
            nc.gpsimd.memset(eps_c[:], EPS).then_inc(const_ready, 1)
            nc.gpsimd.memset(zrow[:], 0.0).then_inc(const_ready, 1)
            pool.wait_ge(const_ready, 9)
            nc.gpsimd.affine_select(out=ident[:], in_=ident[:], compare_op=ALU.not_equal, fill=1.0, base=0,
                                    pattern=[[-1, P]], channel_multiplier=1).then_inc(const_ready, 1)
            pool.wait_ge(const_ready, 10)
            nc.gpsimd.affine_select(out=tri[:], in_=tri[:], compare_op=ALU.is_gt, fill=0.0, base=0,
                                    pattern=[[1, P]], channel_multiplier=-1).then_inc(const_ready, 1)
            for q in range(NQ):
                m = mask[q * QUAD:(q + 1) * QUAD, :]
                pool.wait_ge(const_ready, 11 + q)
                nc.gpsimd.affine_select(out=m, in_=m, compare_op=ALU.is_ge, fill=MASKED, base=0,
                                        pattern=[[-1, QUAD]], channel_multiplier=1).then_inc(const_ready, 1)
            for q in range(NQ):
                m = mask[q * QUAD:(q + 1) * QUAD, 0:SEQ]
                pool.wait_ge(const_ready, 15 + q)
                nc.gpsimd.affine_select(out=m, in_=m, compare_op=ALU.is_gt, fill=MASKED, base=SEQ,
                                        pattern=[[0, SEQ]], channel_multiplier=-1).then_inc(const_ready, 1)
            pool.wait_ge(const_ready, 19)
            nc.gpsimd.tensor_copy(iota[:], iotai[:]).then_inc(const_ready, 1)
            pool.wait_ge(const_ready, 20)
            nc.gpsimd.tensor_copy(prow[:, 0:1], prowi[:]).then_inc(const_ready, 1)
            pool.wait_ge(table_ready, 1)
            n_blocks = pool.value_load(nbi[0:1, 0:1], min_val=E, max_val=BLOCKS)

            def stored(b):
                pool.wait_ge(y_stored[b % 2], 16 * (b // 2 + 1))

            for b in range(E - 2, BLOCKS):
                guarded(pool, n_blocks, b, stored)
            pool.wait_ge(slots_ready, 1)
            for t in range(TT):
                for k in range(TOPK):
                    nc.gpsimd.indirect_dma_start(
                        out=ysel[:, k, t, :], out_offset=None, in_=slot_rows,
                        in_offset=bass.IndirectOffsetOnAxis(ap=sloti[:, k, t:t + 1], axis=0),
                        bounds_check=BLOCKS * P - 1, oob_is_err=True).then_inc(ysel_loaded[t], 16)

        @block.scalar
        def _(act):
            act.dma_start(bo_sb[:], bo.partition_broadcast(P)).then_inc(small_loaded, 16)
            act.dma_start(gw_sb[:], gate_w.rearrange("(c p) e -> p c e", p=P)).then_inc(small_loaded, 16)
            act.dma_start(gb_sb[:], gate_b.partition_broadcast(P)).then_inc(small_loaded, 16)
            act.wait_ge(const_ready, CONSTS)
            act.dma_start(slot_rows[E * P:BLOCKS * P, :].rearrange("(b p) h -> p b h", p=P),
                          zrow[:].rearrange("p (a h) -> p a h", a=1).broadcast_to([P, OVER, H])).then_inc(rows_zeroed, 16)

            def deviation(n):
                t = n % TT
                act.wait_ge(var_ready, n + 1)
                nc.scalar.activation(lnv[:, t:t + 1], mv[:, t, 1:2], ACT.Ln, bias=eps_c[:]).then_inc(ln_ready, 1)
                act.wait_ge(ln_ready, n + 1)
                nc.scalar.activation(rough[:, t:t + 1], lnv[:, t:t + 1], ACT.Exp, scale=-0.5).then_inc(rough_ready, 1)

            def transposed_out(n, bank):
                act.wait_ge(nTp_done, n + 1)
                t = n % TT
                nc.scalar.activation(nT[:, :, t * P:(t + 1) * P], bank[:, t % 2, 0:HC * P].rearrange("p (c n) -> p c n", c=HC),
                                     ACT.Copy).then_inc(nT_ready, 1)

            for t in range(TT):
                act.wait_ge(tok_done, t + 1)
                nc.scalar.activation(hbuf[:, t], psA[:, t % 2, 0:H], ACT.Copy, scale=SCALE).then_inc(h_ready, 1)
                deviation(t)
            for t in range(TT):
                transposed_out(t, psB)
            for c in range(IC):
                act.wait_ge(q_done, c + 1)
                nc.scalar.activation(qT[:, c], psC[:, 2 * (c % 2), :], ACT.Copy, scale=BETA).then_inc(q_evac, 1)

            def exponentials(t):
                act.wait_ge(sub_ready, t + 1)
                nc.scalar.activation(sc[:, t % 2], sc[:, t % 2], ACT.Exp).then_inc(exp_ready, 1)

            def heads_out(t):
                act.wait_ge(pv_done, t + 1)
                if t >= 2:
                    act.wait_ge(oTp_done, t - 1)
                nc.scalar.activation(o_tok[:, t % 2].rearrange("p (a n) -> p a n", a=2), psC[:, 2:4, :], ACT.Copy).then_inc(o_ready, 1)

            exponentials(0)
            exponentials(1)
            heads_out(0)
            exponentials(2)
            heads_out(1)
            deviation(TT)
            exponentials(3)
            heads_out(2)
            deviation(TT + 1)
            heads_out(3)
            deviation(TT + 2)
            transposed_out(TT, psA)
            transposed_out(TT + 1, psA)
            transposed_out(TT + 2, psA)
            deviation(TT + 3)
            transposed_out(TT + 3, psA)
            act.wait_ge(prob_step, 1)
            nc.scalar.activation(gth[:], gdiff[:], ACT.Tanh, scale=0.5).then_inc(gth_ready, 1)

            def x_out(b):
                act.wait_ge(gat_done, b // 2 + 1)
                nc.scalar.activation(xT[:].rearrange("p c n -> p (c n)"), p_gat, ACT.Copy).then_inc(xT_ready, 1)

            def x2_out(b, par):
                act.wait_ge(up_done, b + 1)
                act.wait_ge(wg_loaded[par], 8 * (b - par) + 16)
                at_least(act, z_ready, b)
                for c in range(FC):
                    nc.scalar.activation(x2s[:, c], p_x2[:, c * P:(c + 1) * P], ACT.Identity, bias=ew[:, par, O_B2 + c:O_B2 + c + 1]
                                         ).then_inc(x2_ready, 1)

            def silu(b, par):
                act.wait_ge(g_done, b + 1)
                act.wait_ge(w3_loaded[par], 16 * (b - par) + 32)
                at_least(act, y_done, b - 1)
                for c in range(FC):
                    nc.scalar.activation(sT[:, par, c], p_g[:, c * P:(c + 1) * P], ACT.Silu, bias=ew[:, par, O_BG + c:O_BG + c + 1]
                                         ).then_inc(s_ready, 1)

            def turn(k, par, n_blocks=None):
                guarded(act, n_blocks, k, x2_out, par)
                if par == 1:
                    guarded(act, n_blocks, k + 1, x_out)
                guarded(act, n_blocks, k - 1, silu, 1 - par)

            x_out(0)
            for k in range(4):
                turn(k, k % 2)
            act.wait_ge(table_ready, 1)
            n_blocks = act.value_load(nbi[0:1, 0:1], min_val=E, max_val=BLOCKS)
            with act.Fori(2, ITERS // 2) as i:
                for par in range(2):
                    turn(2 * i + par, par, n_blocks)

        @block.vector
        def _(dve):
            def layer_norm(n, source_ready, source_count):
                t = n % TT
                dve.wait_ge(source_ready, source_count)
                nc.vector.bn_stats(stats[:, t], hbuf[:, t]).then_inc(stats_done, 1)
                dve.wait_ge(stats_done, n + 1)
                nc.vector.bn_aggr(mv[:, t], stats[:, t]).then_inc(var_ready, 1)

            def layer_norm_end(n):
                t = n % TT
                r, a, b = rough[:, t:t + 1], newton[:, t, 0:1], newton[:, t, 1:2]
                dve.wait_ge(var_ready, n + 1)
                nc.vector.tensor_scalar(a, mv[:, t, 1:2], EPS, None, ALU.add).then_inc(newton_ready, 1)
                dve.wait_ge(newton_ready, 3 * n + 1)
                dve.wait_ge(rough_ready, n + 1)
                nc.vector.scalar_tensor_tensor(b, r, a, r, ALU.mult, ALU.mult).then_inc(newton_ready, 1)
                dve.wait_ge(newton_ready, 3 * n + 2)
                nc.vector.tensor_scalar(a, b, -0.5, 1.5, ALU.mult, ALU.add).then_inc(newton_ready, 1)
                dve.wait_ge(newton_ready, 3 * n + 3)
                nc.vector.tensor_tensor(rstd[:, t:t + 1], r, a, ALU.mult).then_inc(rstd_ready, 1)
                dve.wait_ge(rstd_ready, n + 1)
                nc.vector.tensor_scalar(nrm[:, t], hbuf[:, t], mv[:, t, 0:1], rstd[:, t:t + 1], ALU.subtract, ALU.mult
                                        ).then_inc(nrm_ready, 1)

            def values_out(t):
                dve.wait_ge(v_done, t + 1)
                nc.vector.tensor_copy(v_sb[:, t], psC[:, 2 * (t % 2):2 * (t % 2) + 2, :].rearrange("p a n -> p (a n)")
                                      ).then_inc(v_evac, 1)

            for t in range(TT):
                layer_norm(t, h_ready, t + 1)
                layer_norm_end(t)
            values_out(0)
            values_out(1)
            dve.wait_ge(small_loaded, 48)
            for t in range(TT):
                nc.vector.tensor_tensor(hbuf[:, t], hbuf[:, t], bo_sb[:], ALU.add).then_inc(hb_ready, 1)
            dve.wait_ge(const_ready, CONSTS)
            nc.vector.tensor_scalar(sbase[:], iota[:, 0:E], float(P), None, ALU.mult).then_inc(route, 1)
            for c in range(IC):
                dve.wait_ge(k_done, c + 1)
                nc.vector.tensor_copy(kT[:, c], psC[:, 2 * (c % 2) + 1, :]).then_inc(k_evac, 1)

            def scores_out(t):
                b = t % 2
                dve.wait_ge(sc_done, t + 1)
                if t >= 2:
                    dve.wait_ge(pT_ready, t - 1)
                nc.vector.tensor_tensor(sc[:, b].rearrange("p (u c) k -> p u c k", u=2),
                                        psA[:, :, 0:IC * QUAD].rearrange("p u (c k) -> p u c k", c=IC),
                                        mask[:].rearrange("p (a b k) -> p a b k", a=1, b=1).broadcast_to([P, 2, IC, QUAD]),
                                        ALU.add).then_inc(sc_evac, 1)
                dve.wait_ge(sc_evac, t + 1)
                nc.vector.tensor_reduce(mx[:, b], sc[:, b], AX.X, ALU.max).then_inc(mx_ready, 1)
                dve.wait_ge(mx_ready, t + 1)
                nc.vector.tensor_tensor(sc[:, b], sc[:, b], mx[:, b].rearrange("p (h a) -> p h a", a=1).broadcast_to([P, HEADS, QUAD]),
                                        ALU.subtract).then_inc(sub_ready, 1)

            def probabilities(t):
                b = t % 2
                dve.wait_ge(exp_ready, t + 1)
                nc.vector.tensor_reduce(rs[:, b], sc[:, b], AX.X, ALU.add).then_inc(rs_ready, 1)
                dve.wait_ge(rs_ready, t + 1)
                nc.vector.reciprocal(rr[:, b], rs[:, b]).then_inc(rr_ready, 1)
                dve.wait_ge(rr_ready, t + 1)
                nc.vector.tensor_tensor(sc[:, b], sc[:, b], rr[:, b].rearrange("p (h a) -> p h a", a=1).broadcast_to([P, HEADS, QUAD]),
                                        ALU.mult).then_inc(p_ready, 1)
                dve.wait_ge(p_ready, t + 1)
                if t >= 2:
                    dve.wait_ge(pv_done, t - 1)
                nc.vector.transpose(pT[:, b].rearrange("p h k -> p (h k)"), sc[:, b].rearrange("p h k -> p (h k)")
                                    ).then_inc(pT_ready, 1)

            def heads_transposed(t):
                dve.wait_ge(oTp_done, t + 1)
                nc.vector.tensor_copy(oT[:, :, t * P:(t + 1) * P].rearrange("p (a c) n -> p a c n", a=2),
                                      psB[:].rearrange("p a (c n) -> p a c n", n=P)).then_inc(oT_ready, 1)

            def hidden_out(t):
                dve.wait_ge(wo_done, t + 1)
                if t == 0:
                    dve.wait_ge(hb_ready, TT)
                nc.vector.tensor_tensor(hbuf[:, t], psC[:, t % 2, 0:H], hbuf[:, t], ALU.add).then_inc(h1_ready, 1)
                layer_norm(TT + t, h1_ready, t + 1)

            def norm_parts(t):
                dve.wait_ge(nrm_ready, TT + t + 1)
                nc.vector.tensor_copy(nrm_parts[:, 0, t], nrm[:, t]).then_inc(nh_ready, 1)
                dve.wait_ge(nh_ready, t + 1)
                nc.vector.tensor_tensor(nrm_parts[:, 1, t], nrm[:, t], nrm_parts[:, 0, t].bitcast(f32), ALU.subtract
                                        ).then_inc(nl_ready, 1)

            scores_out(0)
            values_out(2)
            probabilities(0)
            scores_out(1)
            values_out(3)
            probabilities(1)
            scores_out(2)
            heads_transposed(0)
            probabilities(2)
            hidden_out(0)
            layer_norm_end(TT)
            norm_parts(0)
            scores_out(3)
            heads_transposed(1)
            probabilities(3)
            hidden_out(1)
            heads_transposed(2)
            layer_norm_end(TT + 1)
            norm_parts(1)
            hidden_out(2)
            heads_transposed(3)
            layer_norm_end(TT + 2)
            norm_parts(2)

            def choose(t0, t1, bank, done):
                n = t1 - t0
                dve.wait_ge(lg_done, done)
                nc.vector.tensor_tensor(lg[:, t0:t1], psB[:, bank, 0:n * E].rearrange("p (t e) -> p t e", t=n),
                                        gb_sb[:].rearrange("p (a e) -> p a e", a=1).broadcast_to([P, n, E]), ALU.add
                                        ).then_inc(lg_ready, n)
                dve.wait_ge(lg_ready, t1)
                for t in range(t0, t1):
                    nc.vector.max(m8[:, t], lg[:, t]).then_inc(m8_ready, 1)
                for t in range(t0, t1):
                    dve.wait_ge(m8_ready, t + 1)
                    nc.vector.max_index(ix8[:, t], m8[:, t], lg[:, t]).then_inc(ix_ready, 1)
                dve.wait_ge(ix_ready, t1)
                nc.vector.tensor_copy(ixf[:, :, t0:t1], ix8[:, t0:t1, 0:TOPK].rearrange("p t k -> p k t")).then_inc(ixf_ready, n)
                dve.wait_ge(ixf_ready, t1)
                for k in range(TOPK):
                    nc.vector.tensor_tensor(pick[:, k, t0:t1], iota[:, 0:E].rearrange("p (a e) -> p a e", a=1).broadcast_to([P, n, E]),
                                            ixf[:, k, t0:t1].rearrange("p (t a) -> p t a", a=1).broadcast_to([P, n, E]),
                                            ALU.is_equal).then_inc(pick_ready, n)
                dve.wait_ge(pick_ready, TOPK * t1)
                nc.vector.tensor_tensor(both[:, t0:t1], pick[:, 0, t0:t1], pick[:, 1, t0:t1], ALU.add).then_inc(both_ready, n)
                dve.wait_ge(both_ready, t1)
                nc.vector.tensor_scalar(absent[:, t0:t1], both[:, t0:t1], -float(2 * TOK), float(2 * TOK), ALU.mult, ALU.add
                                        ).then_inc(absent_ready, n)

            choose(0, TT - 1, 0, 1)
            hidden_out(3)
            layer_norm_end(TT + 3)
            norm_parts(3)
            choose(TT - 1, TT, 1, 2)

            chain = [1]

            def step(instruction):
                chain[0] += 1
                instruction.then_inc(route, 1)
                dve.wait_ge(route, chain[0])

            cumulated = psC[:, 2, 0:TT * E].rearrange("p (t e) -> p t e", t=TT)

            def over_experts(tile):
                return tile.rearrange("p (a e) -> p a e", a=1).broadcast_to([P, TT, E])

            def of_token(slots):
                for k in range(TOPK):
                    nc.vector.tensor_tensor(pickslot[:, k], pick[:, k], slots, ALU.mult).then_inc(route, 1)
                    chain[0] += 1
                dve.wait_ge(route, chain[0])

            dve.wait_ge(cum_done, 1)
            dve.wait_ge(absent_ready, TT)
            nc.vector.tensor_tensor(rank[:], cumulated, absent[:], ALU.add).then_inc(rank_ready, 1)

            def build_onehot(b, par):
                dve.wait_ge(rank_ready, 1)
                at_least(dve, gat_done, b // 2)
                nc.vector.tensor_copy(rank_b[:, par], rank[:, :, bass.ds(b, 1)].rearrange("p t a -> p (t a)")).then_inc(rel_ready, 1)
                dve.wait_ge(rel_ready, b + 1)
                for t in range(TT):
                    nc.vector.tensor_scalar(onehot[:, t, par * P:(par + 1) * P], iota[:], rank_b[:, par, t:t + 1], None, ALU.is_equal
                                            ).then_inc(hot_ready, 1)

            def build_over_onehot(b, par):
                dve.wait_ge(rel_ready, b + 1)
                dve.wait_ge(gat_done, b // 2)
                for t in range(TT):
                    nc.vector.tensor_scalar(onehot[:, t, par * P:(par + 1) * P], iota[:], rel[:, 0, t:t + 1], None, ALU.is_equal
                                            ).then_inc(hot_part, 1)
                for t in range(TT):
                    dve.wait_ge(hot_part, TT * (b - E) + t + 1)
                    nc.vector.scalar_tensor_tensor(onehot[:, t, par * P:(par + 1) * P], iota[:], rel[:, 1, t:t + 1], onehot[:, t, par * P:(par + 1) * P].bitcast(f32),
                                                   ALU.is_equal, ALU.add).then_inc(hot_ready, 1)
                dve.wait_ge(hot_ready, TT * (b + 1))
                nc.vector.tensor_scalar(rel[:], rel[:], -float(P), None, ALU.add).then_inc(rel_ready, 1)

            def gated(b, par):
                dve.wait_ge(up_done, b + 1)
                at_least(dve, g_done, b - 1)
                for c in range(FC):
                    dve.wait_ge(x2_ready, FC * b + c + 1)
                    multiplied = nc.vector.scalar_tensor_tensor(zT[:, par, c], p_x1[:, c * P:(c + 1) * P], ew[:, par, O_B1 + c:O_B1 + c + 1],
                                                                x2s[:, c], ALU.add, ALU.mult)
                multiplied.then_inc(z_ready, 1)

            def y_out(b, par):
                dve.wait_ge(y_done, b + 1)
                dve.wait_ge(w3_loaded[par], 16 * (b - par) + 32)
                if not fixed(b) or b >= 2:
                    dve.wait_ge(y_stored[par], 8 * (b - par))
                nc.vector.tensor_tensor(ysb[:, par], p_y, b3_sb[:, par], ALU.add).then_inc(y_ready, 1)

            def pair_of(b, onehots):
                onehots(b, 0)
                onehots(b + 1, 1)

            def turn(k, par, onehots, n_blocks=None):
                guarded(dve, n_blocks, k, gated, par)
                if par == 0:
                    guarded(dve, n_blocks, k + 2, pair_of, onehots)
                guarded(dve, n_blocks, k - 2, y_out, par)

            build_onehot(0, 0)
            build_onehot(1, 1)
            step(nc.vector.tensor_copy(pos[:, TT], psC[:, 2, TT * E:(TT + 1) * E]))
            count = pos[:, TT]
            step(nc.vector.tensor_scalar(wk8[:, 0], count, float(P), None, ALU.is_gt))
            step(nc.vector.scalar_tensor_tensor(wk8[:, 1], count, float(2 * P), wk8[:, 0], ALU.is_gt, ALU.add))
            step(nc.vector.scalar_tensor_tensor(wk8[:, 2], count, float(3 * P), wk8[:, 1], ALU.is_gt, ALU.add))
            step(nc.vector.tensor_tensor_scan(cum[:], wk8[:, 2], zero8[:], 0.0, ALU.add, ALU.add))
            step(nc.vector.tensor_scalar(nbf[:], cum[:, E - 1:E], float(E), None, ALU.add))
            nc.vector.tensor_copy(nbi[:], nbf[:]).then_inc(route, 1)
            chain[0] += 1
            nc.vector.tensor_copy(etab[:, 0:E], iota[:, 0:E]).then_inc(route, 1)
            chain[0] += 1
            step(nc.vector.tensor_tensor(jle[:], cum[:].rearrange("p (a e) -> p a e", a=1).broadcast_to([P, EXTRA, E]),
                                         iota[:, 0:EXTRA].rearrange("p (j a) -> p j a", a=1).broadcast_to([P, EXTRA, E]), ALU.is_le))
            step(nc.vector.tensor_reduce(etab[:, E:E + EXTRA], jle[:], AX.X, ALU.add))
            step(nc.vector.tensor_scalar(etab[:], etab[:], float(E - 1), None, ALU.min))
            nc.vector.tensor_copy(etabi[:], etab[:]).then_inc(table_ready, 1)
            step(nc.vector.tensor_tensor(obase[:], cum[:], wk8[:, 2], ALU.subtract))
            step(nc.vector.tensor_scalar(obase[:], obase[:], float(P), float((E - 1) * P), ALU.mult, ALU.add))
            step(nc.vector.tensor_tensor(obase[:], obase[:], sbase[:], ALU.subtract))
            step(nc.vector.tensor_scalar(over8[:], cumulated, float(P), None, ALU.is_ge))
            step(nc.vector.tensor_tensor(over8[:], over8[:], over_experts(obase[:]), ALU.mult))
            step(nc.vector.tensor_tensor(pos[:, 0:TT], cumulated, over_experts(sbase[:]), ALU.add))
            step(nc.vector.tensor_tensor(slot8[:], pos[:, 0:TT], over8[:], ALU.add))
            of_token(slot8[:])
            step(nc.vector.tensor_reduce(slotf[:], pickslot[:], AX.X, ALU.add))
            nc.vector.tensor_copy(sloti[:], slotf[:]).then_inc(slots_ready, 1)
            nc.vector.tensor_tensor(gdiff[:], m8[:, :, 0], m8[:, :, 1], ALU.subtract).then_inc(prob_step, 1)
            n_blocks = dve.value_load(nbi[0:1, 0:1], min_val=E, max_val=BLOCKS)
            for k in range(4):
                turn(k, k % 2, build_onehot)
            with dve.Fori(2, E // 2 - 1) as i:
                for par in range(2):
                    turn(2 * i + par, par, build_onehot, n_blocks)
            nc.vector.tensor_scalar(rel[:], slotf[:], -float(E * P), None, ALU.add).then_inc(rel_ready, 1)
            with dve.Fori(E // 2 - 1, ITERS // 2) as i:
                for par in range(2):
                    turn(2 * i + par, par, build_over_onehot, n_blocks)
            guarded(dve, n_blocks, BLOCKS - 1, y_out, (BLOCKS - 1) % 2)
            dve.wait_ge(gth_ready, 1)
            nc.vector.tensor_scalar(prob[:, 0], gth[:], 0.5, 0.5, ALU.mult, ALU.add).then_inc(prob_step, 1)
            nc.vector.tensor_scalar(prob[:, 1], gth[:], -0.5, 0.5, ALU.mult, ALU.add).then_inc(prob_step, 1)
            dve.wait_ge(prob_step, 3)
            for t in range(TT):
                dve.wait_ge(ysel_loaded[t], 16 * TOPK)
                nc.vector.scalar_tensor_tensor(hbuf[:, t], ysel[:, 0, t], prob[:, 0, t:t + 1], hbuf[:, t], ALU.mult, ALU.add
                                               ).then_inc(mix_ready, 1)
                dve.wait_ge(mix_ready, t + 1)
                nc.vector.scalar_tensor_tensor(hbuf[:, t], ysel[:, 1, t], prob[:, 1, t:t + 1], hbuf[:, t], ALU.mult, ALU.add
                                               ).then_inc(out_ready, 1)

        @block.tensor
        def _(pe):
            mm = nc.tensor.matmul
            pe.wait_ge(tw_loaded, 16)
            for t in range(TT):
                pe.wait_ge(x_loaded[t], 16)
                if t >= 2:
                    pe.wait_ge(h_ready, t - 1)
                for c in range(DC):
                    last = mm(psA[:, t % 2, 0:H], x_sb[:, t, c], tw_sb[:, c], start=(c == 0), stop=(c == DC - 1))
                last.then_inc(tok_done, 1)
            pe.wait_ge(const_ready, CONSTS)

            def transposes(n, bank):
                t = n % TT
                pe.wait_ge(nrm_ready, n + 1)
                if n >= 2:
                    pe.wait_ge(nT_ready, n - 1)
                for c in range(HC):
                    last = nc.tensor.transpose(bank[:, t % 2, c * P:(c + 1) * P], nrm[:, t, c * P:(c + 1) * P], ident[:])
                last.then_inc(nTp_done, 1)

            def values(t):
                pe.wait_ge(nT_ready, t + 1)
                if t >= 2:
                    pe.wait_ge(q_evac, IC - 3 + t)
                    pe.wait_ge(k_evac, IC - 3 + t)
                for a in range(2):
                    for c in range(HC):
                        last = mm(psC[:, 2 * (t % 2) + a, :], nT[:, c, t * P:(t + 1) * P],
                                  wv_sb[:, c, a * 512:(a + 1) * 512], start=(c == 0), stop=(c == HC - 1))
                last.then_inc(v_done, 1)

            transposes(0, psB)
            pe.wait_ge(wv_loaded, 16)
            transposes(1, psB)
            values(0)
            transposes(2, psB)
            values(1)
            transposes(3, psB)
            pe.wait_ge(nT_ready, TT)

            def project(c, w, bank, done, evacuated):
                if c < 2:
                    pe.wait_ge(v_evac, 1 + c)
                else:
                    pe.wait_ge(evacuated, c - 1)
                for a in range(HC):
                    last = mm(psC[:, bank, :], w[:, a, c * P:(c + 1) * P], nT[:, a, :], start=(a == 0), stop=(a == HC - 1))
                last.then_inc(done, 1)

            pe.wait_ge(wq_loaded, 16)
            pe.wait_ge(wk_loaded, 16)
            for c in range(IC):
                project(c, wq_sb, 2 * (c % 2), q_done, q_evac)
                project(c, wk_sb, 2 * (c % 2) + 1, k_done, k_evac)

            def scores(t):
                if t == 0:
                    pe.wait_ge(q_evac, IC)
                    pe.wait_ge(k_evac, IC)
                else:
                    pe.wait_ge(sc_evac, t)
                for c in range(IC):
                    for j in range(NQ):
                        tok = slice(t * P + j * QUAD, t * P + (j + 1) * QUAD)
                        for u in range(2):
                            last = mm(psA[j * QUAD:(j + 1) * QUAD, u, c * QUAD:(c + 1) * QUAD],
                                      qT[u * DH:(u + 1) * DH, c, tok], kT[u * DH:(u + 1) * DH, c, tok], start=True, stop=True)
                last.then_inc(sc_done, 1)

            def weigh_values(t):
                pe.wait_ge(pT_ready, t + 1)
                if t == 0:
                    pe.wait_ge(v_evac, TT)
                else:
                    pe.wait_ge(o_ready, t)
                for j in range(NQ):
                    quad = slice(j * QUAD, (j + 1) * QUAD)
                    for h in range(HEADS):
                        last = mm(psC[quad, 2 + h // IC, (h % IC) * DH:(h % IC + 1) * DH],
                                  pT[quad, t % 2, (h % 2) * IC + h // 2, :], v_sb[quad, t, h * DH:(h + 1) * DH],
                                  start=True, stop=True)
                last.then_inc(pv_done, 1)

            def transpose_heads(t):
                pe.wait_ge(o_ready, t + 1)
                if t >= 1:
                    pe.wait_ge(oT_ready, t)
                for c in range(IC):
                    last = nc.tensor.transpose(psB[:, c // 4, (c % 4) * P:(c % 4 + 1) * P], o_tok[:, t % 2, c * P:(c + 1) * P], ident[:])
                last.then_inc(oTp_done, 1)

            def project_out(t):
                pe.wait_ge(oT_ready, t + 1)
                if t >= 2:
                    pe.wait_ge(h1_ready, t - 1)
                for c in range(IC):
                    last = mm(psC[:, t % 2, 0:H], oT[:, c, t * P:(t + 1) * P], wo_sb[:, c], start=(c == 0), stop=(c == IC - 1))
                last.then_inc(wo_done, 1)

            def logits(t0, t1, bank):
                pe.wait_ge(nT_ready, TT + t1)
                for t in range(t0, t1):
                    for c in range(HC):
                        last = mm(psB[:, bank, (t - t0) * E:(t - t0 + 1) * E], nT[:, c, t * P:(t + 1) * P], gw_sb[:, c],
                                  start=(c == 0), stop=(c == HC - 1))
                last.then_inc(lg_done, 1)

            scores(0)
            values(2)
            scores(1)
            values(3)
            pe.wait_ge(wo_loaded, 16)
            weigh_values(0)
            scores(2)
            transpose_heads(0)
            weigh_values(1)
            project_out(0)
            scores(3)
            transpose_heads(1)
            weigh_values(2)
            project_out(1)
            transpose_heads(2)
            weigh_values(3)
            project_out(2)
            pe.wait_ge(sc_evac, TT)
            pe.wait_ge(small_loaded, 48)
            transposes(TT, psA)
            transpose_heads(3)
            transposes(TT + 1, psA)
            project_out(3)
            transposes(TT + 2, psA)
            logits(0, TT - 1, 0)
            transposes(TT + 3, psA)
            logits(TT - 1, TT, 1)
            for t in range(TT + 1):
                pe.wait_ge(both_ready, min(t + 1, TT))
                for a in range(min(t + 1, TT)):
                    last = mm(psC[:, 2, t * E:(t + 1) * E], tri[:] if a == t else ones[:], both[:, a],
                              start=(a == 0), stop=(a == min(t, TT - 1)))
            last.then_inc(cum_done, 1)

            def gather(b):
                pe.wait_ge(hot_ready, TT * (b + 2))
                if fixed(b) and b == 0:
                    pe.wait_ge(nl_ready, TT)
                at_least(pe, xT_ready, b // 2)
                for c in range(HC):
                    for part in range(2):
                        for t in range(TT):
                            last = mm(p_gat[:, c * 2 * P:(c + 1) * 2 * P], nrm_parts[:, part, t, c * P:(c + 1) * P], onehot[:, t],
                                      start=(part == 0 and t == 0), stop=(part == 1 and t == TT - 1))
                last.then_inc(gat_done, 1)

            def up(b, par):
                pe.wait_ge(xT_ready, (b - par) // 2 + 1)
                pe.wait_ge(w12_loaded[par], 8 * (b - par) + 16)
                at_least(pe, z_ready, b)
                for bank, matrix in ((p_x2, O_W2), (p_x1, O_W1)):
                    for f in range(FC):
                        for c in range(HC):
                            at = matrix + c * F + f * P
                            last = mm(bank[:, f * P:(f + 1) * P], ew[:, par, at:at + P], xT[:, c, par * P:(par + 1) * P],
                                      start=(c == 0), stop=(c == HC - 1))
                last.then_inc(up_done, 1)

            def gate(b, par):
                pe.wait_ge(z_ready, b + 1)
                pe.wait_ge(wg_loaded[par], 8 * (b - par) + 16)
                at_least(pe, s_ready, FC * b)
                for g in range(FC):
                    for c in range(FC):
                        at = O_WG + c * F + g * P
                        last = mm(p_g[:, g * P:(g + 1) * P], ew[:, par, at:at + P], zT[:, par, c], start=(c == 0), stop=(c == FC - 1))
                last.then_inc(g_done, 1)

            def down(b, par):
                pe.wait_ge(s_ready, FC * (b + 1))
                pe.wait_ge(w3_loaded[par], 16 * (b - par) + 32)
                at_least(pe, y_ready, b)
                for c in range(FC):
                    last = mm(p_y, sT[:, par, c], ew[:, par, O_W3 + c * H:O_W3 + (c + 1) * H], start=(c == 0), stop=(c == FC - 1))
                last.then_inc(y_done, 1)

            def turn(k, par, n_blocks=None):
                guarded(pe, n_blocks, k, up, par)
                guarded(pe, n_blocks, k - 2, down, par)
                if par == 1:
                    guarded(pe, n_blocks, k + 1, gather)
                guarded(pe, n_blocks, k - 1, gate, 1 - par)

            gather(0)
            for k in range(4):
                turn(k, k % 2)
            pe.wait_ge(table_ready, 1)
            n_blocks = pe.value_load(nbi[0:1, 0:1], min_val=E, max_val=BLOCKS)
            with pe.Fori(2, ITERS // 2) as i:
                for par in range(2):
                    turn(2 * i + par, par, n_blocks)
            guarded(pe, n_blocks, BLOCKS - 1, down, (BLOCKS - 1) % 2)


def kernel(**inputs):
    import numpy as _np
    import concourse.bacc as _bacc
    from concourse import mybir as _mybir
    from concourse.bass_utils import run_bass_kernel_spmd as _run

    P, PATCH = 128, 16
    x = _np.asarray(inputs["x"])
    n, height, width, chans = x.shape
    rows, cols = height // PATCH, width // PATCH
    pt = x.reshape(n, rows, PATCH, cols, PATCH, chans).transpose(0, 1, 3, 2, 4, 5).reshape(n * rows * cols, -1)
    tokens, d = pt.shape
    pt = pt.reshape(tokens // P, P, d // P, P).transpose(0, 3, 2, 1)
    e, h, f = inputs["L0_ffn_w1"].shape

    def chunks(name):
        w = _np.asarray(inputs["L0_ffn_" + name])
        return w.reshape(e, w.shape[1] // P, P, w.shape[2]).transpose(0, 2, 1, 3).reshape(e, P, -1)

    def columns(name):
        return _np.asarray(inputs["L0_ffn_" + name]).reshape(e, -1, P).transpose(0, 2, 1)

    laid = {
        "patches": pt,
        "tok_w": _np.asarray(inputs["L0_tok_weight"]).T,
        "wq": inputs["L0_attn_Wq"], "wk": inputs["L0_attn_Wk"], "wv": inputs["L0_attn_Wv"],
        "wo": inputs["L0_attn_Wo"], "bo": inputs["L0_attn_bo"],
        "gate_w": inputs["L0_ffn_gate_w"], "gate_b": inputs["L0_ffn_gate_b"],
        "expert_w": _np.concatenate([chunks("w1"), chunks("w2"), chunks("wg"), columns("b1"), columns("b2"), chunks("w3"),
                                     columns("bg")], axis=2),
        "b3": inputs["L0_ffn_b3"],
    }
    nc = _bacc.Bacc("TRN2", target_bir_lowering=False, num_devices=1)
    arrays, args = {}, []
    for name, a in laid.items():
        a = _np.ascontiguousarray(a)
        arrays[f"in_{name}"] = a
        args.append(nc.dram_tensor(f"in_{name}", a.shape, _mybir.dt.from_np(a.dtype), kind="ExternalInput").ap())
    blocks = e + (2 * tokens - 1) // P
    args.append(nc.dram_tensor("slot_rows", (blocks * P, h), _mybir.dt.float32, kind="Internal").ap())
    args.append(nc.dram_tensor("out_0", (tokens, h), _mybir.dt.float32, kind="ExternalOutput").ap())
    vit_block_kernel(nc, *args, f)
    r = _run(nc, [arrays], core_ids=[0])
    return r.results[0]["out_0"].reshape(n, rows * cols, h)
```

```python
import concourse.bass as bass
from concourse import mybir
from contextlib import ExitStack


def vit_block_kernel(
    nc: bass.Bass,
    patches: bass.AP,
    tok_w: bass.AP,
    wq: bass.AP,
    wk: bass.AP,
    wv: bass.AP,
    wo: bass.AP,
    bo: bass.AP,
    gate_w: bass.AP,
    gate_b: bass.AP,
    expert_w: bass.AP,
    b3: bass.AP,
    slot_rows: bass.AP,
    out: bass.AP,
    ffn: int,
):
    f32 = mybir.dt.float32
    f32r = mybir.dt.float32r
    bf16 = mybir.dt.bfloat16
    i32 = mybir.dt.int32
    u32 = mybir.dt.uint32
    ALU = mybir.AluOpType
    ACT = mybir.ActivationFunctionType
    AX = mybir.AxisListType

    P = 128
    TT, _, DC, _ = patches.shape
    TOK = TT * P
    H = tok_w.shape[1]
    HC = H // P
    INNER = wq.shape[1]
    DH = 64
    HEADS = INNER // DH
    IC = INNER // P
    SEQ = 16
    QUAD = 32
    NQ = P // QUAD
    E = gate_w.shape[1]
    TOPK = 2
    F = ffn
    FC = F // P
    EW = expert_w.shape[2]
    O_W1, O_W2, O_WG = 0, HC * F, 2 * HC * F
    O_B1 = O_WG + FC * F
    O_B2 = O_B1 + FC
    O_BG = O_B2 + FC
    O_W3 = O_BG + FC
    OVER = (TOK * TOPK - 1) // P
    BLOCKS = E + OVER
    ITERS = BLOCKS + 1
    EXTRA = ITERS + 2 - E
    SCALE = 1.0 / ((1.0 / H ** 0.5) * (DC * P) ** 0.5)
    EPS = 1e-5
    BETA = 1.0 / DH ** 0.5
    MASKED = -3.0e38
    CONSTS = 11 + 2 * NQ

    ctx = ExitStack()
    with ctx:
        def sb(name, shape, dt=f32):
            return ctx.enter_context(nc.sbuf_tensor(name, shape, dt))

        def sem(name):
            return ctx.enter_context(nc.semaphore(name))

        early = sb("early", [P, DC * (TOK + H)])
        x_sb = early[:, 0:DC * TOK].rearrange("p (t c n) -> p t c n", t=TT, c=DC)
        tw_sb = early[:, DC * TOK:DC * (TOK + H)].rearrange("p (c h) -> p c h", c=DC)
        x2s = early[:, 0:F].rearrange("p (c n) -> p c n", c=FC)
        zT, sT = (early[:, a * F:(a + 2) * F].rearrange("p (b c n) -> p b c n", b=2, c=FC) for a in (1, 3))
        o_tok = early[:, 0:2 * INNER].rearrange("p (a n) -> p a n", a=2)
        ysb = early[:, 5 * F:5 * F + 2 * H].rearrange("p (a h) -> p a h", a=2)
        wv_parts = sb("wv_parts", [P, 2, HC, INNER], f32r)
        wo_sb = sb("wo_sb", [P, IC, H])
        qT = sb("qT", [P, IC, TOK])
        kT = sb("kT", [P, IC, TOK])
        v_sb = sb("v_sb", [P, TT, INNER])
        oT = sb("oT", [P, IC, TOK])
        ysel = qT[:, 0:TOPK * TT * H // TOK, :].rearrange("p a n -> p (a n)").rearrange("p (k t h) -> p k t h", k=TOPK, t=TT)
        bo_sb = sb("bo_sb", [P, H])
        gw_sb = sb("gw_sb", [P, HC, E])
        gb_sb = sb("gb_sb", [P, E])
        b3_sb = sb("b3_sb", [P, 2, H])
        hbuf = sb("hbuf", [P, TT, H])
        nrm = sb("nrm", [P, TT, H])
        stats = sb("stats", [P, TT, 6])
        mv = sb("mv", [P, TT, 2])
        root = sb("root", [P, TT])
        halved = sb("halved", [P, TT])
        newton = sb("newton", [P, TT, 2])
        rstd = sb("rstd", [P, TT])
        nT = sb("nT", [P, HC, TOK])
        mask = sb("mask", [P, QUAD])
        sc = sb("sc", [P, TT, HEADS, QUAD])
        mx = sb("mx", [P, TT, HEADS])
        rs = sb("rs", [P, TT, HEADS])
        rr = sb("rr", [P, TT, HEADS])
        pT = sb("pT", [P, 2, HEADS, QUAD])
        ident = sb("ident", [P, P])
        lg = sb("lg", [P, TT, E])
        m8 = sb("m8", [P, TT, 8])
        ix8 = sb("ix8", [P, TT, 8], u32)
        ixf = sb("ixf", [P, TOPK, TT])
        iotai = sb("iotai", [P, P], i32)
        iota = sb("iota", [P, P])
        pick = sb("pick", [P, TOPK, TT, E])
        both = sb("both", [P, TT, E], bf16)
        absent = sb("absent", [P, TT, E])
        tri = sb("tri", [P, P], bf16)
        ones = sb("ones", [P, P], bf16)
        pos = sb("pos", [P, TT + 1, E])
        more = sb("more", [P, 3, E])
        zero8 = sb("zero8", [P, E])
        cum = sb("cum", [P, E])
        sbase = sb("sbase", [P, E])
        obase = sb("obase", [P, E])
        slot8 = sb("slot8", [P, TT, E])
        over8 = sb("over8", [P, TT, E])
        pickslot = sb("pickslot", [P, TOPK, TT, E])
        slotf = sb("slotf", [P, TOPK, TT])
        sloti = sb("sloti", [P, TOPK, TT], u32)
        jle = sb("jle", [P, EXTRA, E])
        etab = sb("etab", [P, E + EXTRA])
        etabi = sb("etabi", [P, E + EXTRA], i32)
        nbf = sb("nbf", [P, 1])
        nbi = sb("nbi", [P, 1], i32)
        gdiff = sb("gdiff", [P, TT])
        gth = sb("gth", [P, TT])
        prob = sb("prob", [P, TOPK, TT])
        rank = sb("rank", [P, TT, E])
        rank_b = sb("rank_b", [P, 2, TT])
        nrm_parts = sb("nrm_parts", [P, 2, TT, H], f32r)
        rel = sb("rel", [P, TOPK, TT])
        onehot = sb("onehot", [P, TT, 2 * P], f32r)
        table_in = sb("table_in", [P, 1])
        eps_c = sb("eps_c", [P, 1])
        zrow = sb("zrow", [P, H])
        xT = sb("xT", [P, HC, 2 * P])
        wv_raw = qT[:, 0:HC * INNER // TOK].rearrange("p a n -> p (a n)").rearrange("p (c n) -> p c n", c=HC)
        wq_raw, wk_raw = (oT[:, a * HC * INNER // TOK:(a + 1) * HC * INNER // TOK].rearrange("p a n -> p (a n)").rearrange("p (c n) -> p c n", c=HC)
                          for a in range(2))
        with nc.sbuf_tensor("wq_parts", [P, 2, HC, INNER], f32r) as wq_parts, \
                nc.sbuf_tensor("wk_parts", [P, 2, HC, INNER], f32r) as wk_parts, \
                nc.sbuf_tensor("nT_parts", [P, 2, HC, TOK], f32r) as nT_parts:
            pass
        ew = sb("ew", [P, 2, EW])

        psA = ctx.enter_context(nc.psum_tensor("psA", [P, 2, 512], f32))
        psB = ctx.enter_context(nc.psum_tensor("psB", [P, 2, 512], f32))
        psC = ctx.enter_context(nc.psum_tensor("psC", [P, 4, 512], f32))
        p_x1, p_x2 = (psA[:, 0, :], psC[:, 1, :]), (psA[:, 1, :], psC[:, 3, :])
        p_gat, p_g, p_y = psB[:, 0, :], psB[:, 1, :], psC[:, 0, 0:H]

        x_loaded = [sem(f"x_loaded{t}") for t in range(TT)]
        x0_loaded, tw_loaded = ([sem(f"{n}{g}") for g in range(3)] for n in ("x0_loaded", "tw_loaded"))
        wv_loaded, wq_loaded, wk_loaded, wo_loaded, small_loaded = (
            sem(n) for n in ("wv_loaded", "wq_loaded", "wk_loaded", "wo_loaded", "small_loaded"))
        w12_loaded, wg_loaded, w3_loaded = ([sem(f"{n}{i}") for i in range(2)] for n in ("w12_loaded", "wg_loaded", "w3_loaded"))
        const_ready = sem("const_ready")
        tok_done, h_ready, stats_done, var_ready, newton_ready, root_ready, rstd_ready, nrm_ready = (
            sem(n) for n in ("tok_done", "h_ready", "stats_done", "var_ready", "newton_ready", "root_ready", "rstd_ready", "nrm_ready"))
        nTp_done, nT_ready, nTh_ready, nTl_ready = (sem(n) for n in ("nTp_done", "nT_ready", "nTh_ready", "nTl_ready"))
        v_done, v_evac, q_done, q_evac, k_done, k_evac = (
            sem(n) for n in ("v_done", "v_evac", "q_done", "q_evac", "k_done", "k_evac"))
        sc_done, sc_evac, mx_ready, sub_ready, exp_ready, rs_ready, rr_ready, p_ready, pT_ready = (
            sem(n) for n in ("sc_done", "sc_evac", "mx_ready", "sub_ready", "exp_ready", "rs_ready", "rr_ready", "p_ready", "pT_ready"))
        pv_done, o_ready, oTp_done, oT_ready, wo_done, hb_ready = (
            sem(n) for n in ("pv_done", "o_ready", "oTp_done", "oT_ready", "wo_done", "hb_ready"))
        lg_done, lg_ready, m8_ready, ix_ready, pick_ready, both_ready, absent_ready = (
            sem(n) for n in ("lg_done", "lg_ready", "m8_ready", "ix_ready", "pick_ready", "both_ready", "absent_ready"))
        cum_done, route, table_ready, slots_ready = (sem(n) for n in ("cum_done", "route", "table_ready", "slots_ready"))
        prob_step, gth_ready = sem("prob_step"), sem("gth_ready")
        wvh_ready, wvl_ready, wqh_ready, wql_ready, wkh_ready, wkl_ready = (
            sem(n) for n in ("wvh_ready", "wvl_ready", "wqh_ready", "wql_ready", "wkh_ready", "wkl_ready"))
        h1_ready, ixf_ready = sem("h1_ready"), sem("ixf_ready")
        rel_ready, hot_part, hot_ready, gat_done, xT_ready, up2_done, up_done, x2_ready, z_ready = (
            sem(n) for n in ("rel_ready", "hot_part", "hot_ready", "gat_done", "xT_ready", "up2_done", "up_done", "x2_ready", "z_ready"))
        g_done, s_ready, y_done, y_ready, rank_ready, nh_ready, nl_ready = (
            sem(n) for n in ("g_done", "s_ready", "y_done", "y_ready", "rank_ready", "nh_ready", "nl_ready"))
        y_stored = [sem(f"y_stored{i}") for i in range(2)]
        ysel_loaded = [sem(f"ysel_loaded{i}") for i in range(TT)]
        rows_zeroed = sem("rows_zeroed")
        mix_ready, out_ready, out_stored = sem("mix_ready"), sem("out_ready"), sem("out_stored")

        block = ctx.enter_context(nc.Block())

        PARTS = ((0, 0), (1, 0), (0, 1))

        def half(weights, a):
            return weights[:, :, a * INNER // 2:(a + 1) * INNER // 2]

        def fixed(b):
            return isinstance(b, int)

        def at_least(engine, signal, count):
            if not fixed(count) or count >= 1:
                engine.wait_ge(signal, count)

        def guarded(engine, n_blocks, block_no, stage, *args):
            if fixed(block_no) and block_no < E:
                if block_no >= 0:
                    stage(block_no, *args)
            else:
                with engine.If(n_blocks > block_no):
                    stage(block_no, *args)

        @block.sync
        def _(sp):
            for g in range(3):
                cs = slice(g * DC // 3, (g + 1) * DC // 3)
                sp.dma_start(x_sb[:, 0, cs], patches[0, :, cs]).then_inc(x0_loaded[g], 16)
                sp.dma_start(tw_sb[:, cs], tok_w[g * DC // 3 * P:(g + 1) * DC // 3 * P].rearrange("(c p) h -> p c h", p=P)
                             ).then_inc(tw_loaded[g], 16)
            for t in range(1, TT):
                sp.dma_start(x_sb[:, t], patches[t]).then_inc(x_loaded[t], 16)
            sp.dma_start(wv_raw, wv.rearrange("(c p) n -> p c n", p=P)).then_inc(wv_loaded, 16)
            sp.dma_start(wq_raw, wq.rearrange("(c p) n -> p c n", p=P)).then_inc(wq_loaded, 16)
            sp.dma_start(wk_raw, wk.rearrange("(c p) n -> p c n", p=P)).then_inc(wk_loaded, 16)
            sp.dma_start(wo_sb[:], wo.rearrange("(c p) n -> p c n", p=P)).then_inc(wo_loaded, 16)

            def expert(b):
                return b if fixed(b) else sp.value_load(etabi[0:1, bass.ds(b, 1)], min_val=0, max_val=E - 1)

            def load(e, par, lo, hi, signal):
                sp.dma_start(ew[:, par, lo:hi], expert_w[bass.ds(e, 1), :, lo:hi].rearrange("e p n -> (e p) n")
                             ).then_inc(signal[par], 16)

            def load_w12(b, par):
                load(expert(b), par, 0, O_WG, w12_loaded)

            def load_wg(b, par):
                load(expert(b), par, O_WG, O_W3, wg_loaded)

            def load_w3(b, par):
                e = expert(b)
                load(e, par, O_W3, EW, w3_loaded)
                sp.dma_start(b3_sb[:, par], b3[bass.ds(e, 1), :].rearrange("e h -> (e h)").partition_broadcast(P)
                             ).then_inc(w3_loaded[par], 16)

            sp.wait_ge(q_done, IC)
            sp.wait_ge(k_done, IC)
            sp.wait_ge(v_done, TT)
            for b in range(2):
                load_w12(b, b)
                load_wg(b, b)
                load_w3(b, b)

            def next_w12(b, par):
                sp.wait_ge(up_done, b - 1)
                load_w12(b, par)

            def next_wg(b, par):
                sp.wait_ge(g_done, b - 1)
                sp.wait_ge(s_ready, b - 1)
                load_wg(b, par)

            def next_w3(b, par):
                sp.wait_ge(y_ready, b - 1)
                load_w3(b, par)

            def store_y(b, par):
                sp.wait_ge(y_ready, b + 1)
                sp.dma_start(slot_rows[bass.ds(b * P, P), :], ysb[:, par]).then_inc(y_stored[par], 16)

            sp.wait_ge(rows_zeroed, 16)

            def turn(k, par, n_blocks=None):
                guarded(sp, n_blocks, k + 2, next_w12, par)
                if not fixed(k) or k >= 1:
                    guarded(sp, n_blocks, k + 1, next_wg, 1 - par)
                guarded(sp, n_blocks, k - 2, store_y, par)
                if not fixed(k) or k >= 2:
                    guarded(sp, n_blocks, k, next_w3, par)

            for k in range(4):
                turn(k, k % 2)
            sp.wait_ge(table_ready, 1)
            n_blocks = sp.value_load(nbi[0:1, 0:1], min_val=E, max_val=BLOCKS)
            with sp.Fori(2, ITERS // 2) as i:
                for par in range(2):
                    turn(2 * i + par, par, n_blocks)
            guarded(sp, n_blocks, BLOCKS - 1, store_y, (BLOCKS - 1) % 2)
            for t in range(TT):
                sp.wait_ge(out_ready, t + 1)
                sp.dma_start(out[t * P:(t + 1) * P, :], hbuf[:, t]).then_inc(out_stored, 16)
            sp.wait_ge(out_stored, 16 * TT)

        @block.gpsimd
        def _(pool):
            nc.gpsimd.memset(ident[:], 0.0).then_inc(const_ready, 1)
            nc.gpsimd.memset(tri[:], 1.0).then_inc(const_ready, 1)
            nc.gpsimd.memset(ones[:], 1.0).then_inc(const_ready, 1)
            nc.gpsimd.memset(mask[:], 0.0).then_inc(const_ready, 1)
            nc.gpsimd.memset(zero8[:], 0.0).then_inc(const_ready, 1)
            nc.gpsimd.iota(iotai[:], pattern=[[1, P]], base=0, channel_multiplier=0).then_inc(const_ready, 1)
            nc.gpsimd.memset(eps_c[:], EPS).then_inc(const_ready, 1)
            nc.gpsimd.memset(zrow[:], 0.0).then_inc(const_ready, 1)
            pool.wait_ge(const_ready, 8)
            nc.gpsimd.affine_select(out=ident[:], in_=ident[:], compare_op=ALU.not_equal, fill=1.0, base=0,
                                    pattern=[[-1, P]], channel_multiplier=1).then_inc(const_ready, 1)
            pool.wait_ge(const_ready, 9)
            nc.gpsimd.affine_select(out=tri[:], in_=tri[:], compare_op=ALU.is_gt, fill=0.0, base=0,
                                    pattern=[[1, P]], channel_multiplier=-1).then_inc(const_ready, 1)
            for q in range(NQ):
                m = mask[q * QUAD:(q + 1) * QUAD, :]
                pool.wait_ge(const_ready, 10 + q)
                nc.gpsimd.affine_select(out=m, in_=m, compare_op=ALU.is_ge, fill=MASKED, base=0,
                                        pattern=[[-1, QUAD]], channel_multiplier=1).then_inc(const_ready, 1)
            for q in range(NQ):
                m = mask[q * QUAD:(q + 1) * QUAD, 0:SEQ]
                pool.wait_ge(const_ready, 10 + NQ + q)
                nc.gpsimd.affine_select(out=m, in_=m, compare_op=ALU.is_gt, fill=MASKED, base=SEQ,
                                        pattern=[[0, SEQ]], channel_multiplier=-1).then_inc(const_ready, 1)
            pool.wait_ge(const_ready, 10 + 2 * NQ)
            nc.gpsimd.tensor_copy(iota[:], iotai[:]).then_inc(const_ready, 1)
            for raw, parts, highs, signal in ((wv_raw, wv_parts, wvh_ready, wvl_ready), (wk_raw, wk_parts, wkh_ready, wkl_ready)):
                for a in range(2):
                    pool.wait_ge(highs, a + 1)
                    nc.gpsimd.tensor_tensor(half(parts[:, 1], a), half(raw, a), half(parts[:, 0], a).bitcast(f32), ALU.subtract
                                            ).then_inc(signal, 1)
            pool.wait_ge(table_ready, 1)
            n_blocks = pool.value_load(nbi[0:1, 0:1], min_val=E, max_val=BLOCKS)

            def stored(b):
                pool.wait_ge(y_stored[b % 2], 16 * (b // 2 + 1))

            for b in range(E - 2, BLOCKS):
                guarded(pool, n_blocks, b, stored)
            pool.wait_ge(slots_ready, 1)
            for t in range(TT):
                for k in range(TOPK):
                    nc.gpsimd.indirect_dma_start(
                        out=ysel[:, k, t, :], out_offset=None, in_=slot_rows,
                        in_offset=bass.IndirectOffsetOnAxis(ap=sloti[:, k, t:t + 1], axis=0),
                        bounds_check=BLOCKS * P - 1, oob_is_err=True).then_inc(ysel_loaded[t], 16)

        @block.scalar
        def _(act):
            act.dma_start(bo_sb[:], bo.partition_broadcast(P)).then_inc(small_loaded, 16)
            act.dma_start(gw_sb[:], gate_w.rearrange("(c p) e -> p c e", p=P)).then_inc(small_loaded, 16)
            act.dma_start(gb_sb[:], gate_b.partition_broadcast(P)).then_inc(small_loaded, 16)
            act.wait_ge(const_ready, CONSTS)
            act.dma_start(slot_rows[E * P:BLOCKS * P, :].rearrange("(b p) h -> p b h", p=P),
                          zrow[:].rearrange("p (a h) -> p a h", a=1).broadcast_to([P, OVER, H])).then_inc(rows_zeroed, 16)

            def transposed_out(t):
                act.wait_ge(nTp_done, TT + t + 1)
                nc.scalar.activation(nT[:, :, t * P:(t + 1) * P], psA[:, t % 2, 0:HC * P].rearrange("p (c n) -> p c n", c=HC),
                                     ACT.Copy).then_inc(nT_ready, 1)

            def weights_high(raw, parts, a, loaded, signal):
                act.wait_ge(loaded, 16)
                nc.scalar.activation(half(parts[:, 0], a), half(raw, a), ACT.Copy).then_inc(signal, 1)

            def transposed_high(t):
                act.wait_ge(nTp_done, t + 1)
                nc.scalar.activation(nT_parts[:, 0, :, t * P:(t + 1) * P], psB[:, t % 2, 0:HC * P].rearrange("p (c n) -> p c n", c=HC),
                                     ACT.Copy).then_inc(nTh_ready, 1)

            def deviation(n):
                t = n % TT
                act.wait_ge(var_ready, n + 1)
                if n >= TT:
                    act.wait_ge(newton_ready, 3 * (n - TT) + 2)
                nc.scalar.activation(root[:, t:t + 1], mv[:, t, 1:2], ACT.Sqrt, bias=eps_c[:]).then_inc(root_ready, 1)

            for t in range(TT):
                act.wait_ge(tok_done, t + 1)
                nc.scalar.activation(hbuf[:, t], psA[:, t % 2, 0:H], ACT.Copy, scale=SCALE).then_inc(h_ready, 1)
                deviation(t)
                if t == 2:
                    weights_high(wv_raw, wv_parts, 0, wv_loaded, wvh_ready)
                    weights_high(wv_raw, wv_parts, 1, wv_loaded, wvh_ready)
            transposed_high(0)
            transposed_high(1)
            transposed_high(2)
            weights_high(wq_raw, wq_parts, 0, wq_loaded, wqh_ready)
            transposed_high(3)
            weights_high(wk_raw, wk_parts, 0, wk_loaded, wkh_ready)
            weights_high(wq_raw, wq_parts, 1, wq_loaded, wqh_ready)
            weights_high(wk_raw, wk_parts, 1, wk_loaded, wkh_ready)
            for c in range(IC):
                act.wait_ge(q_done, c + 1)
                nc.scalar.activation(qT[:, c], psC[:, 2 - 2 * (c % 2), :], ACT.Copy, scale=BETA).then_inc(q_evac, 1)

            nc.scalar.activation(table_in[:], eps_c[:], ACT.Exp)

            def exponentials(t):
                act.wait_ge(sub_ready, t + 1)
                nc.scalar.activation(sc[:, t], sc[:, t], ACT.Exp).then_inc(exp_ready, 1)

            def heads_out(t):
                act.wait_ge(pv_done, t + 1)
                at_least(act, oTp_done, t - 1)
                nc.scalar.activation(o_tok[:, t % 2, 0:512], psC[:, 2, :], ACT.Copy).then_inc(o_ready, 1)

            def heads_transposed(t):
                act.wait_ge(oTp_done, t + 1)
                nc.scalar.activation(oT[:, 0:4, t * P:(t + 1) * P], psB[:, 0, :].rearrange("p (c n) -> p c n", c=4), ACT.Copy
                                     ).then_inc(oT_ready, 1)

            def values_out(t, bank):
                act.wait_ge(v_done, t + 1)
                nc.scalar.activation(v_sb[:, t], psC[:, bank:bank + 2, :].rearrange("p a n -> p (a n)"), ACT.Copy
                                     ).then_inc(v_evac, 1)

            exponentials(0)
            values_out(1, 2)
            values_out(2, 0)
            exponentials(1)
            exponentials(2)
            heads_out(0)
            values_out(3, 0)
            exponentials(3)
            heads_transposed(0)
            heads_out(1)
            deviation(TT)
            heads_transposed(1)
            heads_out(2)
            deviation(TT + 1)
            heads_transposed(2)
            heads_out(3)
            transposed_out(0)
            transposed_out(1)
            deviation(TT + 2)
            heads_transposed(3)
            transposed_out(2)
            deviation(TT + 3)
            transposed_out(3)

            def x_out(b):
                act.wait_ge(gat_done, b // 2 + 1)
                nc.scalar.activation(xT[:].rearrange("p c n -> p (c n)"), p_gat, ACT.Copy).then_inc(xT_ready, 1)

            def x2_out(b, par):
                act.wait_ge(up2_done, b + 1)
                act.wait_ge(wg_loaded[par], 8 * (b - par) + 16)
                at_least(act, z_ready, b)
                for c in range(FC):
                    nc.scalar.activation(x2s[:, c], p_x2[par][:, c * P:(c + 1) * P], ACT.Identity, bias=ew[:, par, O_B2 + c:O_B2 + c + 1]
                                         ).then_inc(x2_ready, 1)

            def silu(b, par):
                act.wait_ge(g_done, b + 1)
                act.wait_ge(wg_loaded[par], 8 * (b - par) + 16)
                at_least(act, y_done, b - 1)
                for c in range(FC):
                    last = nc.scalar.activation(sT[:, par, c], p_g[:, c * P:(c + 1) * P], ACT.Silu, bias=ew[:, par, O_BG + c:O_BG + c + 1])
                last.then_inc(s_ready, 1)

            def turn(k, par, n_blocks=None):
                guarded(act, n_blocks, k, x2_out, par)
                if par == 1:
                    guarded(act, n_blocks, k + 1, x_out)
                guarded(act, n_blocks, k - 1, silu, 1 - par)

            x_out(0)
            for k in range(4):
                turn(k, k % 2)
            act.wait_ge(prob_step, 1)
            nc.scalar.activation(gth[:], gdiff[:], ACT.Tanh, scale=0.5).then_inc(gth_ready, 1)
            act.wait_ge(table_ready, 1)
            n_blocks = act.value_load(nbi[0:1, 0:1], min_val=E, max_val=BLOCKS)
            with act.Fori(2, ITERS // 2) as i:
                for par in range(2):
                    turn(2 * i + par, par, n_blocks)

        @block.vector
        def _(dve):
            def mean_and_variance(n, source_ready, source_count):
                t = n % TT
                dve.wait_ge(source_ready, source_count)
                nc.vector.bn_stats(stats[:, t], hbuf[:, t]).then_inc(stats_done, 1)
                dve.wait_ge(stats_done, n + 1)
                nc.vector.bn_aggr(mv[:, t], stats[:, t]).then_inc(var_ready, 1)

            def normalize(n):
                t = n % TT
                guess, square = newton[:, t, 0:1], newton[:, t, 1:2]
                dve.wait_ge(var_ready, n + 1)
                nc.vector.tensor_scalar(halved[:, t:t + 1], mv[:, t, 1:2], -0.5, -0.5 * EPS, ALU.mult, ALU.add).then_inc(newton_ready, 1)
                dve.wait_ge(root_ready, n + 1)
                nc.vector.reciprocal(guess, root[:, t:t + 1]).then_inc(newton_ready, 1)
                dve.wait_ge(newton_ready, 3 * n + 2)
                nc.vector.scalar_tensor_tensor(square, guess, halved[:, t:t + 1], guess, ALU.mult, ALU.mult).then_inc(newton_ready, 1)
                dve.wait_ge(newton_ready, 3 * n + 3)
                nc.vector.scalar_tensor_tensor(rstd[:, t:t + 1], square, 1.5, guess, ALU.add, ALU.mult).then_inc(rstd_ready, 1)
                dve.wait_ge(rstd_ready, n + 1)
                nc.vector.tensor_scalar(nrm[:, t], hbuf[:, t], mv[:, t, 0:1], rstd[:, t:t + 1], ALU.subtract, ALU.mult
                                        ).then_inc(nrm_ready, 1)

            def values_out(t):
                dve.wait_ge(v_done, t + 1)
                nc.vector.tensor_copy(v_sb[:, t], psC[:, 2 * (t % 2):2 * (t % 2) + 2, :].rearrange("p a n -> p (a n)")
                                      ).then_inc(v_evac, 1)

            def transposed_low(t):
                dve.wait_ge(nTh_ready, t + 1)
                at = slice(t * P, (t + 1) * P)
                nc.vector.tensor_tensor(nT_parts[:, 1, :, at], psB[:, t % 2, 0:HC * P].rearrange("p (c n) -> p c n", c=HC),
                                        nT_parts[:, 0, :, at].bitcast(f32), ALU.subtract).then_inc(nTl_ready, 1)

            def wq_low(a):
                dve.wait_ge(wqh_ready, a + 1)
                nc.vector.tensor_tensor(half(wq_parts[:, 1], a), half(wq_raw, a), half(wq_parts[:, 0], a).bitcast(f32), ALU.subtract
                                        ).then_inc(wql_ready, 1)

            for t in range(TT):
                mean_and_variance(t, h_ready, t + 1)
                normalize(t)
            transposed_low(0)
            transposed_low(1)
            transposed_low(2)
            wq_low(0)
            transposed_low(3)
            wq_low(1)
            values_out(0)
            dve.wait_ge(small_loaded, 48)
            for t in range(TT):
                nc.vector.tensor_tensor(hbuf[:, t], hbuf[:, t], bo_sb[:], ALU.add).then_inc(hb_ready, 1)
            dve.wait_ge(const_ready, CONSTS)
            nc.vector.tensor_scalar(sbase[:], iota[:, 0:E], float(P), None, ALU.mult).then_inc(route, 1)
            for c in range(IC):
                dve.wait_ge(k_done, c + 1)
                nc.vector.tensor_copy(kT[:, c], psC[:, 3 - 2 * (c % 2), :]).then_inc(k_evac, 1)

            def scores_out(t):
                dve.wait_ge(sc_done, 1)
                nc.vector.tensor_tensor(sc[:, t].rearrange("p (u c) k -> p u c k", u=2),
                                        (psA, psB)[t // 2][:, :, t % 2 * IC * QUAD:(t % 2 + 1) * IC * QUAD].rearrange("p u (c k) -> p u c k", c=IC),
                                        mask[:].rearrange("p (a b k) -> p a b k", a=1, b=1).broadcast_to([P, 2, IC, QUAD]),
                                        ALU.add).then_inc(sc_evac, 1)

            def shift(t):
                dve.wait_ge(sc_evac, t + 1)
                nc.vector.tensor_reduce(mx[:, t], sc[:, t], AX.X, ALU.max).then_inc(mx_ready, 1)
                dve.wait_ge(mx_ready, t + 1)
                nc.vector.tensor_tensor(sc[:, t], sc[:, t], mx[:, t].rearrange("p (h a) -> p h a", a=1).broadcast_to([P, HEADS, QUAD]),
                                        ALU.subtract).then_inc(sub_ready, 1)

            def probabilities(t):
                dve.wait_ge(exp_ready, t + 1)
                nc.vector.tensor_reduce(rs[:, t], sc[:, t], AX.X, ALU.add).then_inc(rs_ready, 1)
                dve.wait_ge(rs_ready, t + 1)
                nc.vector.reciprocal(rr[:, t], rs[:, t]).then_inc(rr_ready, 1)
                dve.wait_ge(rr_ready, t + 1)
                nc.vector.tensor_tensor(sc[:, t], sc[:, t], rr[:, t].rearrange("p (h a) -> p h a", a=1).broadcast_to([P, HEADS, QUAD]),
                                        ALU.mult).then_inc(p_ready, 1)
                dve.wait_ge(p_ready, t + 1)
                at_least(dve, pv_done, t - 1)
                nc.vector.transpose(pT[:, t % 2].rearrange("p h k -> p (h k)"), sc[:, t].rearrange("p h k -> p (h k)")
                                    ).then_inc(pT_ready, 1)

            def heads_out(t):
                dve.wait_ge(pv_done, t + 1)
                at_least(dve, oTp_done, t - 1)
                nc.vector.tensor_copy(o_tok[:, t % 2, 512:1024], psC[:, 3, :]).then_inc(o_ready, 1)

            def heads_transposed(t):
                dve.wait_ge(oTp_done, t + 1)
                nc.vector.tensor_copy(oT[:, 4:8, t * P:(t + 1) * P], psB[:, 1, :].rearrange("p (c n) -> p c n", c=4)
                                      ).then_inc(oT_ready, 1)

            def hidden_out(t):
                dve.wait_ge(wo_done, t + 1)
                if t == 0:
                    dve.wait_ge(hb_ready, TT)
                nc.vector.tensor_tensor(hbuf[:, t], psC[:, t % 2, 0:H], hbuf[:, t], ALU.add).then_inc(h1_ready, 1)
                mean_and_variance(TT + t, h1_ready, t + 1)

            def norm_parts(t):
                dve.wait_ge(nrm_ready, TT + t + 1)
                nc.vector.tensor_copy(nrm_parts[:, 0, t], nrm[:, t]).then_inc(nh_ready, 1)
                dve.wait_ge(nh_ready, t + 1)
                nc.vector.tensor_tensor(nrm_parts[:, 1, t], nrm[:, t], nrm_parts[:, 0, t].bitcast(f32), ALU.subtract
                                        ).then_inc(nl_ready, 1)

            scores_out(0)
            shift(0)
            scores_out(1)
            probabilities(0)
            shift(1)
            scores_out(2)
            probabilities(1)
            shift(2)
            scores_out(3)
            heads_out(0)
            shift(3)
            heads_transposed(0)
            probabilities(2)
            heads_out(1)
            probabilities(3)
            for t in range(TT - 1):
                hidden_out(t)
                heads_transposed(t + 1)
                normalize(TT + t)
                norm_parts(t)
                if t + 2 < TT:
                    heads_out(t + 2)

            def choose(t0, t1):
                n = t1 - t0
                dve.wait_ge(lg_done, t1 // (TT // 2))
                nc.vector.tensor_tensor(lg[:, t0:t1], psC[:, 3, t0 * E:t1 * E].rearrange("p (t e) -> p t e", t=n),
                                        gb_sb[:].rearrange("p (a e) -> p a e", a=1).broadcast_to([P, n, E]), ALU.add
                                        ).then_inc(lg_ready, n)
                dve.wait_ge(lg_ready, t1)
                for t in range(t0, t1):
                    nc.vector.max(m8[:, t], lg[:, t]).then_inc(m8_ready, 1)
                for t in range(t0, t1):
                    dve.wait_ge(m8_ready, t + 1)
                    nc.vector.max_index(ix8[:, t], m8[:, t], lg[:, t]).then_inc(ix_ready, 1)
                dve.wait_ge(ix_ready, t1)
                nc.vector.tensor_copy(ixf[:, :, t0:t1], ix8[:, t0:t1, 0:TOPK].rearrange("p t k -> p k t")).then_inc(ixf_ready, n)
                dve.wait_ge(ixf_ready, t1)
                for k in range(TOPK):
                    nc.vector.tensor_tensor(pick[:, k, t0:t1], iota[:, 0:E].rearrange("p (a e) -> p a e", a=1).broadcast_to([P, n, E]),
                                            ixf[:, k, t0:t1].rearrange("p (t a) -> p t a", a=1).broadcast_to([P, n, E]),
                                            ALU.is_equal).then_inc(pick_ready, n)
                dve.wait_ge(pick_ready, TOPK * t1)
                nc.vector.tensor_tensor(both[:, t0:t1], pick[:, 0, t0:t1], pick[:, 1, t0:t1], ALU.add).then_inc(both_ready, n)
                dve.wait_ge(both_ready, t1)
                nc.vector.tensor_scalar(absent[:, t0:t1], both[:, t0:t1], -float(2 * TOK), float(2 * TOK), ALU.mult, ALU.add
                                        ).then_inc(absent_ready, n)

            choose(0, TT // 2)
            hidden_out(3)
            normalize(TT + 3)
            norm_parts(3)
            choose(TT // 2, TT)

            chain = [1]

            def step(instruction):
                chain[0] += 1
                instruction.then_inc(route, 1)
                dve.wait_ge(route, chain[0])

            cumulated = psC[:, 2, 0:TT * E].rearrange("p (t e) -> p t e", t=TT)

            def over_experts(tile):
                return tile.rearrange("p (a e) -> p a e", a=1).broadcast_to([P, TT, E])

            def of_token(slots):
                for k in range(TOPK):
                    nc.vector.tensor_tensor(pickslot[:, k], pick[:, k], slots, ALU.mult).then_inc(route, 1)
                    chain[0] += 1
                dve.wait_ge(route, chain[0])

            dve.wait_ge(cum_done, 1)
            dve.wait_ge(absent_ready, TT)
            nc.vector.tensor_tensor(rank[:], cumulated, absent[:], ALU.add).then_inc(rank_ready, 1)

            def build_onehot(b, par):
                dve.wait_ge(rank_ready, 1)
                at_least(dve, gat_done, b // 2)
                nc.vector.tensor_copy(rank_b[:, par], rank[:, :, bass.ds(b, 1)].rearrange("p t a -> p (t a)")).then_inc(rel_ready, 1)
                dve.wait_ge(rel_ready, b + 1)
                for t in range(TT):
                    nc.vector.tensor_scalar(onehot[:, t, par * P:(par + 1) * P], iota[:], rank_b[:, par, t:t + 1], None, ALU.is_equal
                                            ).then_inc(hot_ready, 1)

            def build_over_onehot(b, par):
                dve.wait_ge(rel_ready, b + 1)
                dve.wait_ge(gat_done, b // 2)
                for t in range(TT):
                    nc.vector.tensor_scalar(onehot[:, t, par * P:(par + 1) * P], iota[:], rel[:, 0, t:t + 1], None, ALU.is_equal
                                            ).then_inc(hot_part, 1)
                for t in range(TT):
                    dve.wait_ge(hot_part, TT * (b - E) + t + 1)
                    hot = onehot[:, t, par * P:(par + 1) * P]
                    nc.vector.scalar_tensor_tensor(hot, iota[:], rel[:, 1, t:t + 1], hot.bitcast(f32), ALU.is_equal, ALU.add).then_inc(hot_ready, 1)
                dve.wait_ge(hot_ready, TT * (b + 1))
                nc.vector.tensor_scalar(rel[:], rel[:], -float(P), None, ALU.add).then_inc(rel_ready, 1)

            def gated(b, par):
                dve.wait_ge(up_done, b + 1)
                at_least(dve, g_done, b - 1)
                for c in range(FC):
                    dve.wait_ge(x2_ready, FC * b + c + 1)
                    multiplied = nc.vector.scalar_tensor_tensor(zT[:, par, c], p_x1[par][:, c * P:(c + 1) * P], ew[:, par, O_B1 + c:O_B1 + c + 1],
                                                                x2s[:, c], ALU.add, ALU.mult)
                multiplied.then_inc(z_ready, 1)

            def y_out(b, par):
                dve.wait_ge(y_done, b + 1)
                dve.wait_ge(w3_loaded[par], 16 * (b - par) + 32)
                if not fixed(b) or b >= 2:
                    dve.wait_ge(y_stored[par], 8 * (b - par))
                nc.vector.tensor_tensor(ysb[:, par], p_y, b3_sb[:, par], ALU.add).then_inc(y_ready, 1)

            def pair_of(b, onehots):
                onehots(b, 0)
                onehots(b + 1, 1)

            def turn(k, par, onehots, n_blocks=None):
                guarded(dve, n_blocks, k, gated, par)
                if par == 0:
                    guarded(dve, n_blocks, k + 2, pair_of, onehots)
                guarded(dve, n_blocks, k - 2, y_out, par)

            build_onehot(0, 0)
            build_onehot(1, 1)
            step(nc.vector.tensor_copy(pos[:, TT], psC[:, 2, TT * E:(TT + 1) * E]))
            count = pos[:, TT]
            step(nc.vector.tensor_scalar(more[:, 0], count, float(P), None, ALU.is_gt))
            step(nc.vector.scalar_tensor_tensor(more[:, 1], count, float(2 * P), more[:, 0], ALU.is_gt, ALU.add))
            step(nc.vector.scalar_tensor_tensor(more[:, 2], count, float(3 * P), more[:, 1], ALU.is_gt, ALU.add))
            step(nc.vector.tensor_tensor_scan(cum[:], more[:, 2], zero8[:], 0.0, ALU.add, ALU.add))
            step(nc.vector.tensor_scalar(nbf[:], cum[:, E - 1:E], float(E), None, ALU.add))
            nc.vector.tensor_copy(nbi[:], nbf[:]).then_inc(route, 1)
            chain[0] += 1
            nc.vector.tensor_copy(etab[:, 0:E], iota[:, 0:E]).then_inc(route, 1)
            chain[0] += 1
            step(nc.vector.tensor_tensor(jle[:], cum[:].rearrange("p (a e) -> p a e", a=1).broadcast_to([P, EXTRA, E]),
                                         iota[:, 0:EXTRA].rearrange("p (j a) -> p j a", a=1).broadcast_to([P, EXTRA, E]), ALU.is_le))
            step(nc.vector.tensor_reduce(etab[:, E:E + EXTRA], jle[:], AX.X, ALU.add))
            step(nc.vector.tensor_scalar(etab[:], etab[:], float(E - 1), None, ALU.min))
            nc.vector.tensor_copy(etabi[:], etab[:]).then_inc(table_ready, 1)
            step(nc.vector.tensor_tensor(obase[:], cum[:], more[:, 2], ALU.subtract))
            step(nc.vector.tensor_scalar(obase[:], obase[:], float(P), float((E - 1) * P), ALU.mult, ALU.add))
            step(nc.vector.tensor_tensor(obase[:], obase[:], sbase[:], ALU.subtract))
            step(nc.vector.tensor_scalar(over8[:], cumulated, float(P), None, ALU.is_ge))
            step(nc.vector.tensor_tensor(over8[:], over8[:], over_experts(obase[:]), ALU.mult))
            step(nc.vector.tensor_tensor(pos[:, 0:TT], cumulated, over_experts(sbase[:]), ALU.add))
            step(nc.vector.tensor_tensor(slot8[:], pos[:, 0:TT], over8[:], ALU.add))
            of_token(slot8[:])
            step(nc.vector.tensor_reduce(slotf[:], pickslot[:], AX.X, ALU.add))
            nc.vector.tensor_copy(sloti[:], slotf[:]).then_inc(slots_ready, 1)
            nc.vector.tensor_tensor(gdiff[:], m8[:, :, 0], m8[:, :, 1], ALU.subtract).then_inc(prob_step, 1)
            n_blocks = dve.value_load(nbi[0:1, 0:1], min_val=E, max_val=BLOCKS)
            for k in range(4):
                turn(k, k % 2, build_onehot)
            with dve.Fori(2, E // 2 - 1) as i:
                for par in range(2):
                    turn(2 * i + par, par, build_onehot, n_blocks)
            nc.vector.tensor_scalar(rel[:], slotf[:], -float(E * P), None, ALU.add).then_inc(rel_ready, 1)
            with dve.Fori(E // 2 - 1, ITERS // 2) as i:
                for par in range(2):
                    turn(2 * i + par, par, build_over_onehot, n_blocks)
            guarded(dve, n_blocks, BLOCKS - 1, y_out, (BLOCKS - 1) % 2)
            dve.wait_ge(gth_ready, 1)
            nc.vector.tensor_scalar(prob[:, 0], gth[:], 0.5, 0.5, ALU.mult, ALU.add).then_inc(prob_step, 1)
            nc.vector.tensor_scalar(prob[:, 1], gth[:], -0.5, 0.5, ALU.mult, ALU.add).then_inc(prob_step, 1)
            dve.wait_ge(prob_step, 3)
            for t in range(TT):
                dve.wait_ge(ysel_loaded[t], 16 * TOPK)
                nc.vector.scalar_tensor_tensor(hbuf[:, t], ysel[:, 0, t], prob[:, 0, t:t + 1], hbuf[:, t], ALU.mult, ALU.add
                                               ).then_inc(mix_ready, 1)
                dve.wait_ge(mix_ready, t + 1)
                nc.vector.scalar_tensor_tensor(hbuf[:, t], ysel[:, 1, t], prob[:, 1, t:t + 1], hbuf[:, t], ALU.mult, ALU.add
                                               ).then_inc(out_ready, 1)

        @block.tensor
        def _(pe):
            mm = nc.tensor.matmul
            for t in range(TT):
                if t >= 1:
                    pe.wait_ge(x_loaded[t], 16)
                if t >= 2:
                    pe.wait_ge(h_ready, t - 1)
                for c in range(DC):
                    if t == 0 and c % (DC // 3) == 0:
                        pe.wait_ge(tw_loaded[c // (DC // 3)], 16)
                        pe.wait_ge(x0_loaded[c // (DC // 3)], 16)
                    last = mm(psA[:, t % 2, 0:H], x_sb[:, t, c], tw_sb[:, c], start=(c == 0), stop=(c == DC - 1))
                last.then_inc(tok_done, 1)
            pe.wait_ge(const_ready, CONSTS)

            def transposes(n, bank):
                t = n % TT
                pe.wait_ge(nrm_ready, n + 1)
                at_least(pe, nTl_ready if n < TT else nT_ready, t - 1)
                for c in range(HC):
                    last = nc.tensor.transpose(bank[:, t % 2, c * P:(c + 1) * P], nrm[:, t, c * P:(c + 1) * P], ident[:])
                last.then_inc(nTp_done, 1)

            def values(t, a):
                bank = 2 * (t == 1) + a
                if a == 0:
                    pe.wait_ge(nTl_ready, t + 1)
                    if t == 1:
                        pe.wait_ge(q_evac, IC - 1)
                        pe.wait_ge(k_evac, IC - 1)
                    if t == 2:
                        pe.wait_ge(q_evac, IC)
                        pe.wait_ge(k_evac, IC)
                    if t == 3:
                        pe.wait_ge(v_evac, 3)
                if t == 0:
                    pe.wait_ge(wvl_ready, a + 1)
                for n, (w, x) in enumerate(PARTS):
                    for c in range(HC):
                        last = mm(psC[:, bank, :], nT_parts[:, x, c, t * P:(t + 1) * P], half(wv_parts[:, w], a)[:, c],
                                  start=(n == 0 and c == 0), stop=(n == 2 and c == HC - 1))
                if a == 1:
                    last.then_inc(v_done, 1)

            for t in range(TT - 1):
                transposes(t, psB)
            values(0, 0)
            transposes(TT - 1, psB)
            values(0, 1)
            pe.wait_ge(nTl_ready, TT)

            def project(c, parts, split, bank, done, evacuated):
                if c == 1:
                    pe.wait_ge(v_evac, 1)
                elif c >= 2:
                    pe.wait_ge(evacuated, c - 1)
                pe.wait_ge(split, 1 if c < IC // 2 else 2)
                for n, (w, x) in enumerate(PARTS):
                    for a in range(HC):
                        last = mm(psC[:, bank, :], parts[:, w, a, c * P:(c + 1) * P], nT_parts[:, x, a, :],
                                  start=(n == 0 and a == 0), stop=(n == 2 and a == HC - 1))
                last.then_inc(done, 1)

            def scores(c):
                pe.wait_ge(q_evac, c + 1)
                pe.wait_ge(k_evac, c + 1)
                if c == 0:
                    pe.wait_ge(h_ready, TT)
                for t in range(TT):
                    for j in range(NQ):
                        tok = slice(t * P + j * QUAD, t * P + (j + 1) * QUAD)
                        for u in range(2):
                            last = mm((psA, psB)[t // 2][j * QUAD:(j + 1) * QUAD, u, (t % 2 * IC + c) * QUAD:(t % 2 * IC + c + 1) * QUAD],
                                      qT[u * DH:(u + 1) * DH, c, tok], kT[u * DH:(u + 1) * DH, c, tok], start=True, stop=True)
                if c == IC - 1:
                    last.then_inc(sc_done, 1)

            for c in range(IC):
                project(c, wq_parts, wql_ready, 2 - 2 * (c % 2), q_done, q_evac)
                project(c, wk_parts, wkl_ready, 3 - 2 * (c % 2), k_done, k_evac)
                if c >= 1:
                    scores(c - 1)

            def weigh_values(t, j):
                if j == 0:
                    pe.wait_ge(pT_ready, t + 1)
                    pe.wait_ge(v_evac, max(t, 1) + 1)
                    at_least(pe, o_ready, 2 * t)
                quad = slice(j * QUAD, (j + 1) * QUAD)
                for h in range(HEADS):
                    last = mm(psC[quad, 2 + h // IC, (h % IC) * DH:(h % IC + 1) * DH],
                              pT[quad, t % 2, (h % 2) * IC + h // 2, :], v_sb[quad, t, h * DH:(h + 1) * DH],
                              start=True, stop=True)
                if j == NQ - 1:
                    last.then_inc(pv_done, 1)

            def transpose_heads(t):
                pe.wait_ge(o_ready, 2 * t + 2)
                if t == 0:
                    pe.wait_ge(sc_evac, TT)
                at_least(pe, oT_ready, 2 * t)
                for c in range(IC):
                    last = nc.tensor.transpose(psB[:, c // 4, (c % 4) * P:(c % 4 + 1) * P], o_tok[:, t % 2, c * P:(c + 1) * P], ident[:])
                last.then_inc(oTp_done, 1)

            def project_out(t, c0, c1):
                if c0 == 0:
                    pe.wait_ge(oT_ready, 2 * t + 2)
                    if t == 0:
                        pe.wait_ge(v_evac, TT)
                        pe.wait_ge(wo_loaded, 16)
                    at_least(pe, h1_ready, t - 1)
                for c in range(c0, c1):
                    last = mm(psC[:, t % 2, 0:H], oT[:, c, t * P:(t + 1) * P], wo_sb[:, c], start=(c == 0), stop=(c == IC - 1))
                if c1 == IC:
                    last.then_inc(wo_done, 1)

            def keep_clock(n):
                for _ in range(n):
                    mm(p_g[:, 0:P], ident[:], ident[:], start=True, stop=True)

            def logits(t0, t1):
                pe.wait_ge(nT_ready, t1)
                for t in range(t0, t1):
                    for c in range(HC):
                        last = mm(psC[:, 3, t * E:(t + 1) * E], nT[:, c, t * P:(t + 1) * P], gw_sb[:, c],
                                  start=(c == 0), stop=(c == HC - 1))
                last.then_inc(lg_done, 1)

            scores(IC - 1)
            values(1, 0)
            values(1, 1)
            values(2, 0)
            values(2, 1)
            for t in range(TT):
                weigh_values(t, 0)
                weigh_values(t, 1)
                if t == 0:
                    values(3, 0)
                if t >= 1:
                    project_out(t - 1, 0, 2)
                weigh_values(t, 2)
                if t >= 1:
                    project_out(t - 1, 2, 4)
                weigh_values(t, 3)
                if t >= 1:
                    project_out(t - 1, 4, 8)
                else:
                    values(3, 1)
                if t == TT - 1:
                    transposes(TT, psA)
                    transposes(TT + 1, psA)
                transpose_heads(t)
            pe.wait_ge(small_loaded, 48)
            logits(0, TT // 2)
            project_out(TT - 1, 0, 3)
            transposes(TT + 2, psA)
            project_out(TT - 1, 3, 8)
            keep_clock(6)
            transposes(TT + 3, psA)
            logits(TT // 2, TT)
            keep_clock(2)
            for t in range(TT + 1):
                if t == TT // 2:
                    keep_clock(3)
                pe.wait_ge(both_ready, min(t + 1, TT))
                for a in range(min(t + 1, TT)):
                    last = mm(psC[:, 2, t * E:(t + 1) * E], tri[:] if a == t else ones[:], both[:, a],
                              start=(a == 0), stop=(a == min(t, TT - 1)))
            last.then_inc(cum_done, 1)

            def gather(b):
                pe.wait_ge(hot_ready, TT * (b + 2))
                if fixed(b) and b == 0:
                    pe.wait_ge(nl_ready, TT)
                at_least(pe, xT_ready, b // 2)
                for c in range(HC):
                    for part in range(2):
                        for t in range(TT):
                            last = mm(p_gat[:, c * 2 * P:(c + 1) * 2 * P], nrm_parts[:, part, t, c * P:(c + 1) * P], onehot[:, t],
                                      start=(part == 0 and t == 0), stop=(part == 1 and t == TT - 1))
                last.then_inc(gat_done, 1)

            def up(b, par):
                pe.wait_ge(xT_ready, (b - par) // 2 + 1)
                pe.wait_ge(w12_loaded[par], 8 * (b - par) + 16)
                at_least(pe, z_ready, b - 1)
                for bank, matrix, done in ((p_x2[par], O_W2, up2_done), (p_x1[par], O_W1, up_done)):
                    for f in range(FC):
                        for c in range(HC):
                            at = matrix + c * F + f * P
                            last = mm(bank[:, f * P:(f + 1) * P], ew[:, par, at:at + P], xT[:, c, par * P:(par + 1) * P],
                                      start=(c == 0), stop=(c == HC - 1))
                    last.then_inc(done, 1)

            def gate(b, par):
                pe.wait_ge(z_ready, b + 1)
                pe.wait_ge(wg_loaded[par], 8 * (b - par) + 16)
                at_least(pe, s_ready, b)
                for g in range(FC):
                    for c in range(FC):
                        at = O_WG + c * F + g * P
                        last = mm(p_g[:, g * P:(g + 1) * P], ew[:, par, at:at + P], zT[:, par, c], start=(c == 0), stop=(c == FC - 1))
                last.then_inc(g_done, 1)

            def down(b, par):
                pe.wait_ge(s_ready, b + 1)
                pe.wait_ge(w3_loaded[par], 16 * (b - par) + 32)
                at_least(pe, y_ready, b)
                for c in range(FC):
                    last = mm(p_y, sT[:, par, c], ew[:, par, O_W3 + c * H:O_W3 + (c + 1) * H], start=(c == 0), stop=(c == FC - 1))
                last.then_inc(y_done, 1)

            def turn(k, par, n_blocks=None):
                guarded(pe, n_blocks, k, up, par)
                if par == 1:
                    guarded(pe, n_blocks, k + 1, gather)
                guarded(pe, n_blocks, k - 1, gate, 1 - par)
                guarded(pe, n_blocks, k - 2, down, par)

            keep_clock(6)
            gather(0)
            for k in range(4):
                turn(k, k % 2)
            pe.wait_ge(table_ready, 1)
            n_blocks = pe.value_load(nbi[0:1, 0:1], min_val=E, max_val=BLOCKS)
            with pe.Fori(2, ITERS // 2) as i:
                for par in range(2):
                    turn(2 * i + par, par, n_blocks)
            guarded(pe, n_blocks, BLOCKS - 1, down, (BLOCKS - 1) % 2)


def kernel(**inputs):
    import numpy as _np
    import concourse.bacc as _bacc
    from concourse import mybir as _mybir
    from concourse.bass_utils import run_bass_kernel_spmd as _run

    P, PATCH = 128, 16
    x = _np.asarray(inputs["x"])
    n, height, width, chans = x.shape
    rows, cols = height // PATCH, width // PATCH
    pt = x.reshape(n, rows, PATCH, cols, PATCH, chans).transpose(0, 1, 3, 2, 4, 5).reshape(n * rows * cols, -1)
    tokens, d = pt.shape
    pt = pt.reshape(tokens // P, P, d // P, P).transpose(0, 3, 2, 1)
    e, h, f = inputs["L0_ffn_w1"].shape

    def chunks(name):
        w = _np.asarray(inputs["L0_ffn_" + name])
        return w.reshape(e, w.shape[1] // P, P, w.shape[2]).transpose(0, 2, 1, 3).reshape(e, P, -1)

    def columns(name):
        return _np.asarray(inputs["L0_ffn_" + name]).reshape(e, -1, P).transpose(0, 2, 1)

    laid = {
        "patches": pt,
        "tok_w": _np.asarray(inputs["L0_tok_weight"]).T,
        "wq": inputs["L0_attn_Wq"], "wk": inputs["L0_attn_Wk"], "wv": inputs["L0_attn_Wv"],
        "wo": inputs["L0_attn_Wo"], "bo": inputs["L0_attn_bo"],
        "gate_w": inputs["L0_ffn_gate_w"], "gate_b": inputs["L0_ffn_gate_b"],
        "expert_w": _np.concatenate([chunks("w1"), chunks("w2"), chunks("wg"), columns("b1"), columns("b2"),
                                     columns("bg"), chunks("w3")], axis=2),
        "b3": inputs["L0_ffn_b3"],
    }
    nc = _bacc.Bacc("TRN2", target_bir_lowering=False, num_devices=1)
    arrays, args = {}, []
    for name, a in laid.items():
        a = _np.ascontiguousarray(a)
        arrays[f"in_{name}"] = a
        args.append(nc.dram_tensor(f"in_{name}", a.shape, _mybir.dt.from_np(a.dtype), kind="ExternalInput").ap())
    blocks = e + (2 * tokens - 1) // P
    args.append(nc.dram_tensor("slot_rows", (blocks * P, h), _mybir.dt.float32, kind="Internal").ap())
    args.append(nc.dram_tensor("out_0", (tokens, h), _mybir.dt.float32, kind="ExternalOutput").ap())
    vit_block_kernel(nc, *args, f)
    r = _run(nc, [arrays], core_ids=[0])
    return r.results[0]["out_0"].reshape(n, rows * cols, h)
```
